# Optimizing a Trainium2 kernel written in Bass

```python
import numpy as np
import jax
import jax.numpy as jnp

def _softmax(x, axis=-1):
    return jax.nn.softmax(x, axis=axis)

def _gelu(x):
    return jax.nn.gelu(x, approximate=True)

def _silu(x):
    return jax.nn.silu(x)

def _sigmoid(x):
    return jax.nn.sigmoid(x)

def _layernorm(x, axis=-1, eps=1e-05):
    m = jnp.mean(x, axis=axis, keepdims=True)
    v = jnp.var(x, axis=axis, keepdims=True)
    return (x - m) / jnp.sqrt(v + eps)

def _scatter_add(tgt, idx, src, axis=0):
    return tgt.at[idx].add(src)

def _segment_sum(src, seg, n):
    return jax.ops.segment_sum(src, seg, n)
kernel_name = 'mk_gnn_preln_d1_gnn_r32_480b9d'

def setup_inputs(seed: int=0):
    np.random.seed(seed)
    _w = jnp.asarray

    def _rec_inputs():
        import jax
        import jax.numpy as jnp
        _gk = jax.random.key(seed)
        x = -0.000202 + 1 * jax.random.normal(jax.random.fold_in(_gk, 1), (50000, 128), jnp.float32)
        src = jax.random.randint(jax.random.fold_in(_gk, 2), (50000,), 0, 50000, jnp.int32)
        dst = jax.random.randint(jax.random.fold_in(_gk, 3), (50000,), 0, 50000, jnp.int32)
        _o = jnp.argsort(dst, stable=True)
        src = src[_o]
        dst = dst[_o]
        edge_type_32 = jax.random.randint(jax.random.fold_in(_gk, 12), (50000,), 0, 32, jnp.int32)
        edge_weight1 = jax.random.uniform(jax.random.fold_in(_gk, 13), (50000, 1), jnp.float32, 0.0, 0.999998)
        return (x, src, dst, edge_type_32, edge_weight1)
    x, src, dst, edge_type_32, edge_weight1 = _rec_inputs()

    def _L0_gnn_setup():
        import jax, jax.numpy as jnp
        import numpy as np
        N, E, D, F, R, B = (50000, 50000, 128, 128, 32, 8)
        key = jax.random.key(seed)
        ks = jax.random.split(key, 9)
        h = jax.random.normal(ks[0], (N, D), dtype=jnp.float32)
        src = jax.random.randint(ks[1], (E,), 0, N, dtype=jnp.int32)
        dst = jax.random.randint(ks[2], (E,), 0, N, dtype=jnp.int32)
        etype = jax.random.randint(ks[3], (E,), 0, R, dtype=jnp.int32)
        norm = jax.random.uniform(ks[4], (E, 1), dtype=jnp.float32)
        weight = jax.random.normal(ks[5], (B, D, F), dtype=jnp.float32) * (2.0 / (D + F)) ** 0.5
        w_comp = jax.random.normal(ks[6], (R, B), dtype=jnp.float32) * (2.0 / (R + B)) ** 0.5
        loop_weight = jax.random.normal(ks[7], (D, F), dtype=jnp.float32) * (2.0 / (D + F)) ** 0.5
        h_bias = jnp.zeros((F,), dtype=jnp.float32)
        return {'h': h, 'src': src, 'dst': dst, 'etype': etype, 'norm': norm, 'weight': weight, 'w_comp': w_comp, 'loop_weight': loop_weight, 'h_bias': h_bias}
    _L0_gnn_all = _L0_gnn_setup()
    _L0_gnn_in = {k: v for k, v in _L0_gnn_all.items() if k in ('weight', 'w_comp', 'loop_weight', 'h_bias')}
    del _L0_gnn_all
    return {'x': x, 'src': src, 'dst': dst, 'edge_type_32': edge_type_32, 'edge_weight1': edge_weight1, 'L0_gnn_weight': _L0_gnn_in['weight'], 'L0_gnn_w_comp': _L0_gnn_in['w_comp'], 'L0_gnn_loop_weight': _L0_gnn_in['loop_weight'], 'L0_gnn_h_bias': _L0_gnn_in['h_bias']}

def reference(x, src, dst, edge_type_32, edge_weight1, L0_gnn_weight, L0_gnn_w_comp, L0_gnn_loop_weight, L0_gnn_h_bias):
    import jax
    import jax.numpy as jnp

    def _L0_gnn_ref(h, src, dst, etype, norm, weight, w_comp, loop_weight, h_bias):
        import jax, jax.numpy as jnp
        import numpy as np
        N, E, D, F, R, B = (50000, 50000, 128, 128, 32, 8)
        n_nodes, d_in = h.shape
        n_rels = w_comp.shape[0]
        W_rel = jnp.einsum('rb,bdf->rdf', w_comp, weight)
        seg = etype * n_nodes + dst
        agg = jax.ops.segment_sum(h[src] * norm, seg, num_segments=n_rels * n_nodes)
        agg = agg.reshape(n_rels, n_nodes, d_in)
        node_repr = jnp.einsum('rnd,rdf->nf', agg, W_rel)
        node_repr = node_repr + h_bias + h @ loop_weight
        return jax.nn.relu(node_repr)
    h = jnp.maximum(_layernorm(x, axis=-1), 0.0)
    x = x + _L0_gnn_ref(h, src, dst, edge_type_32, edge_weight1, L0_gnn_weight, L0_gnn_w_comp, L0_gnn_loop_weight, L0_gnn_h_bias)
    return x

_drawn_inputs = setup_inputs


def setup_inputs(seed=0):
    import zlib

    import numpy as np

    out = dict(_drawn_inputs(seed))
    spreads = {'L0_gnn_h_bias': (0.0, 0.1)}
    factors = {}
    for name, (base, spread) in spreads.items():
        noise = np.random.default_rng([zlib.crc32(name.encode()), seed]).standard_normal(out[name].shape)
        drawn = base * np.exp(spread * noise) if base else spread * noise
        out[name] = jnp.asarray(drawn.astype(out[name].dtype))
    for name, factor in factors.items():
        out[name] = (out[name] * factor).astype(out[name].dtype)
    return out
```

```python
from contextlib import ExitStack

import numpy as np

import concourse.bass as bass
from concourse import mybir

ALU = mybir.AluOpType
ACT = mybir.ActivationFunctionType
F32 = mybir.dt.float32
BF16 = mybir.dt.bfloat16
I32 = mybir.dt.int32
AX_X = mybir.AxisListType.X

P = 128
G = 4
RING = 3
EPS = 1e-5
CHUNKS = 2
NRING = 4
SEG_P = 96


def sweep(eng, count, step, ring=RING, peel=5):
    for g in range(min(peel, count)):
        step(g, g // ring, g % ring)
    rounds = max(0, (count - peel) // ring)
    if rounds:
        with eng.Fori(0, rounds) as i:
            for k in range(peel, peel + ring):
                step(i * ring + k, i + k // ring, k % ring)
    for g in range(peel + ring * rounds, count):
        step(g, g // ring, g % ring)


def hold(eng, passed):
    eng.sem_inc(passed, 1)


def round_before(n, q, k=1, ring=RING):
    return n + (q - k) // ring


def round_after(n, q, ring=RING):
    return n + (q + 1) // ring


def beyond(g, n):
    return isinstance(g, int) and g >= n


def is_before(g, n):
    return isinstance(g, int) and g < n


def build_layer(nc, x, src, dst, etype, norm, weight, w_comp, loop_weight, bias, out):
    N, D = x.shape
    E = src.shape[0]
    R, B = w_comp.shape
    F = loop_weight.shape[1]
    NT = -(-E // P)
    NT = -(-NT // G) * G
    NG = NT // G
    EP = NT * P
    FULL_P, REST = E // NT, E % NT
    NW = -(-N // P)
    LAST = N - (NW - 1) * P
    NGW = -(-NW // G)
    SEG = SEG_P * CHUNKS
    LO = 32
    HI = -(-(NW + 1) // LO)
    DST_PAD = HI * LO * P - 1
    NODE_ROWS = (NW + 1) * P
    DUMMY = EP + NODE_ROWS
    ROWS = DUMMY + P
    C = F + 1
    assert D == P and F == P and R * G == P and 2 * G * P <= 1024 and B == 8
    assert REST > 0 and EP - E <= SEG and NG > RING and NGW > RING

    msgs = nc.dram_tensor("msgs", [ROWS, C], F32, kind="Internal").ap()
    first_row = nc.dram_tensor("first_row", [HI * LO, 1], I32, kind="Internal").ap()
    mode = nc.dram_tensor("mode", [1, 1], I32, kind="Internal").ap()

    ctx = ExitStack()
    with ctx:
        def sb(name, shape, dt=F32):
            return ctx.enter_context(nc.sbuf_tensor(name, shape, dt))

        def psum(name, shape, dt=F32):
            return ctx.enter_context(nc.psum_tensor(name, shape, dt))

        def sem(name):
            return ctx.enter_context(nc.semaphore(name))

        iota_i = sb("iota_i", [P, P], I32)
        part_i = sb("part_i", [P, 1], I32)
        iota_n = sb("iota_n", [P, P])
        part_f = sb("part_f", [P, 1])
        ident = sb("ident", [P, P])
        above = sb("above", [P, P])
        below = sb("below", [P, P])
        ones = sb("ones", [P, P])
        eps_col = sb("eps_col", [P, 1])
        win_i = sb("win_i", [P, NGW * G], I32)
        win_off = sb("win_off", [P, NGW * G])
        w_all = sb("w_all", [P, B, F])
        w_loop = sb("w_loop", [P, F])
        w_mix = sb("w_mix", [P, G * B])
        src_all = sb("src_all", [P, NT], I32)
        type_i = sb("type_i", [P, NT], I32)
        type_f = sb("type_f", [P, NT])
        norm_all = sb("norm_all", [P, NT])
        dst_i = sb("dst_i", [P, NT], I32)
        dst_f = sb("dst_f", [P, NT])
        next_i = sb("next_i", [P, 1], I32)
        next_f = sb("next_f", [P, 1])
        hi_i = sb("hi_i", [P, NT], I32)
        lo_i = sb("lo_i", [P, NT], I32)
        hi_f = sb("hi_f", [P, NT])
        lo_f = sb("lo_f", [P, NT])
        hi_hot = sb("hi_hot", [P, NT, HI], BF16)
        lo_hot = sb("lo_hot", [P, NT, LO], BF16)
        falls = sb("falls", [P, NT])
        bad = sb("bad", [P, 4])
        hist = sb("hist", [HI, LO])
        upto = sb("upto", [HI, LO])
        start = sb("start", [HI, LO])
        start_c = sb("start_c", [HI, LO])
        start_i = sb("start_i", [HI, LO], I32)
        big = sb("big", [HI, LO])
        row_tab = sb("row_tab", [1, HI * LO], I32)
        mode_f = sb("mode_f", [P, 1])
        mode_i = sb("mode_i", [P, 1], I32)
        xg = sb("xg", [P, RING, G, D])
        stats = sb("stats", [P, RING, G, 6])
        mv = sb("mv", [P, RING, G, 2])
        neg_mean = sb("neg_mean", [P, RING, G])
        std = sb("std", [P, RING, G])
        rstd = sb("rstd", [P, RING, G])
        h = sb("h", [P, RING, G, D])
        hT = sb("hT", [P, RING, G, P])
        idx = sb("idx", [P, RING, G], I32)
        hot = sb("hot", [P, RING, G, R])
        hotT = sb("hotT", [P, RING, P])
        gain = sb("gain", [P, RING, G])
        mix = sb("mix", [P, RING, G, B])
        z = sb("z", [P, RING, 3, F])
        u = sb("u", [P, RING, F])
        sum_a = sb("sum_a", [P, RING, F])
        sum_b = sb("sum_b", [P, RING, F])
        msg = sb("msg", [P, RING, G, C])
        xw = sb("xw", [P, NRING, G, D])
        nstats = sb("nstats", [P, NRING, G, 6])
        nmv = sb("nmv", [P, NRING, G, 2])
        nstd = sb("nstd", [P, NRING, G])
        nrstd = sb("nrstd", [P, NRING, G])
        shift = sb("shift", [P, NRING, G])
        hw = sb("hw", [P, NRING, G, D])
        hwT = sb("hwT", [P, NRING, G, P])
        seg = sb("seg", [P, NRING, G, CHUNKS, C])
        rel = sb("rel", [SEG_P, NRING, G, CHUNKS])
        pick = sb("pick", [P, NRING, G, CHUNKS, P])
        res = sb("res", [P, NRING, G, F])
        cz = sb("cz", [P, C])
        cm = sb("cm", [P, C])
        ccur = sb("ccur", [P, C])
        cdst = sb("cdst", [P, P])
        ceq = sb("ceq", [P, P])
        cwork = sb("cwork", [P, P])
        cc = sb("cc", [P, 8])
        cidx = sb("cidx", [P, 1], I32)

        y_ps = [psum(f"y_ps{r}", [P, B, F]) for r in range(RING)]
        hT_ps = psum("hT_ps", [P, G, P])
        mix_ps = psum("mix_ps", [P, 512])

        win_ps = [y_ps[0][:, 0:G, :], y_ps[1][:, 0:G, :], y_ps[2][:, 0:G, :], y_ps[0][:, G:2 * G, :]]
        hwT_ps = [hT_ps[:, :, :], mix_ps[:, :].rearrange("p (t e) -> p t e", t=G)]

        s_cst = sem("s_cst")
        passed = {e: sem(f"passed_{e}") for e in ("sp", "pool", "dve")}
        s_clr = sem("s_clr")
        s_num = sem("s_num")
        s_src = sem("s_src")
        s_ld = sem("s_ld")
        s_wt = sem("s_wt")
        s_con = sem("s_con")
        s_meta = sem("s_meta")
        s_hist = sem("s_hist")
        s_start = sem("s_start")
        s_off = sem("s_off")
        s_tab = sem("s_tab")
        s_idx = sem("s_idx")
        s_gather = [sem(f"s_gather{i}") for i in range(RING * G)]
        s_bn = sem("s_bn")
        s_mean = sem("s_mean")
        s_hot = sem("s_hot")
        s_std = sem("s_std")
        s_small = sem("s_small")
        s_mix = sem("s_mix")
        s_relu = sem("s_relu")
        s_hotT = sem("s_hotT")
        s_hotT_sb = sem("s_hotT_sb")
        s_mix_ps = sem("s_mix_ps")
        s_hT = sem("s_hT")
        s_hT_sb = sem("s_hT_sb")
        s_y_high = sem("s_y_high")
        s_y = sem("s_y")
        s_z_high = sem("s_z_high")
        s_z = sem("s_z")
        s_u = sem("s_u")
        s_a = sem("s_a")
        s_b = sem("s_b")
        s_msg = sem("s_msg")
        s_dcol = sem("s_dcol")
        s_mst = [sem(f"s_mst{q}") for q in range(RING)]
        c_zero = sem("c_zero")
        c_zst = sem("c_zst")
        c_ld = sem("c_ld")
        c_dst = sem("c_dst")
        c_row = sem("c_row")
        c_v = sem("c_v")
        c_sum = sem("c_sum")
        c_idx = sem("c_idx")
        c_cur = sem("c_cur")
        c_new = sem("c_new")
        c_own = sem("c_own")
        c_st = sem("c_st")
        n_x = [sem(f"n_x{q}") for q in range(NRING)]
        n_seg = [sem(f"n_seg{q}") for q in range(NRING)]
        n_bn = sem("n_bn")
        n_mv = sem("n_mv")
        n_std = sem("n_std")
        n_rstd = sem("n_rstd")
        n_shift = sem("n_shift")
        n_h = sem("n_h")
        n_pick = sem("n_pick")
        n_rel = sem("n_rel")
        n_hT = sem("n_hT")
        n_hT_sb = sem("n_hT_sb")
        n_y = sem("n_y")
        n_res = sem("n_res")
        n_out = [sem(f"n_out{q}") for q in range(NRING)]

        def edges(a):
            return (a[0:FULL_P * NT].rearrange("(p t) -> p t", t=NT),
                    a[FULL_P * NT:E].rearrange("(p t) -> p t", p=1))

        def load_edges(eng, tile, a, s):
            full, rest = edges(a)
            eng.dma_start(tile[0:FULL_P, :], full).then_inc(s, 16)
            eng.dma_start(tile[FULL_P:FULL_P + 1, 0:REST], rest).then_inc(s, 16)

        msg_rows = msgs[0:EP, :].rearrange("(p t) c -> p (t c)", t=NT)
        start_flat = first_row.rearrange("(a b) c -> a (b c)", b=LO)
        X_WIN = x[0:(NW - 1) * P, :].rearrange("(w p) d -> p w d", p=P)
        OUT_WIN = out[0:(NW - 1) * P, :].rearrange("(w p) d -> p w d", p=P)
        LAST_FULL = NW - 1 - (NGW - 1) * G

        block = ctx.enter_context(nc.Block())

        @block.sync
        def _(sp):
            sp.wait_ge(s_clr, 1)
            load_edges(sp, src_all, src, s_src)
            sp.wait_ge(s_clr, 6)
            load_edges(sp, dst_i, dst, s_ld)
            sp.dma_start(next_i[0:FULL_P - 1, :],
                         dst[NT:FULL_P * NT].rearrange("(p t) -> p t", t=NT)[:, 0:1],
                         allow_slow_non_contiguous=True).then_inc(s_ld, 16)
            sp.dma_start(next_i[FULL_P - 1:FULL_P, :],
                         dst[FULL_P * NT:FULL_P * NT + 1].rearrange("(p t) -> p t", p=1)).then_inc(s_ld, 16)
            load_edges(sp, type_i, etype, s_ld)
            load_edges(sp, norm_all, norm.rearrange("e o -> (e o)"), s_ld)
            sp.dma_start(w_all[:, :, :], weight.rearrange("b d f -> d b f")).then_inc(s_wt, 16)
            sp.dma_start(w_loop[:, :], loop_weight).then_inc(s_wt, 16)
            for j in range(G):
                sp.dma_start(w_mix[R * j:R * j + R, B * j:B * j + B], w_comp).then_inc(s_wt, 16)
            sp.dma_start(seg[SEG_P:SEG_P + 1, :, :, CHUNKS - 1, 0:F].rearrange("p q j f -> p (q j) f"),
                         bias.rearrange("(a b f) -> a b f", a=1, b=1).to_broadcast([1, NRING * G, F])).then_inc(s_wt, 16)

            def store_messages(g, n, q):
                sp.wait_ge(s_msg, g * G + G)
                hold(sp, passed["sp"])
                sp.wait_ge(s_dcol, g + 1)
                hold(sp, passed["sp"])
                sp.dma_start(msg_rows[:, bass.ds(g * (G * C), G * C)],
                             msg[:, q, :, :].rearrange("p t c -> p (t c)")).then_inc(s_mst[q], 16)

            sp.wait_ge(s_start, 1)
            sp.dma_start(start_flat, start_i[:, :]).then_inc(s_tab, 16)
            sp.dma_start(mode, mode_i[0:1, :]).then_inc(s_tab, 16)
            sp.wait_ge(s_tab, 32)
            sp.dma_start(row_tab[:, :], first_row.rearrange("w c -> c w")).then_inc(s_tab, 16)
            sweep(sp, NG, store_messages)
            for q in range(RING):
                sp.wait_ge(s_mst[q], 16 * len(range(q, NG, RING)))

            sp.wait_ge(s_tab, 48)
            with sp.If(sp.value_load(mode, min_val=0, max_val=1) > 0):
                with sp.Fori(0, NW + 2) as w:
                    sp.wait_ge(c_zero, w + 1)
                    hold(sp, passed["sp"])
                    sp.dma_start(msgs[bass.ds(w * P + EP, P), :], cz[:, :]).then_inc(c_zst, 16)
                with sp.Fori(0, NT) as t:
                    sp.dma_start(cm[:, :], msgs[bass.ds(t * P, P), :]).then_inc(c_ld, 16)
                    sp.wait_ge(c_st, t * 16 + 16)
                    hold(sp, passed["sp"])

            def load_windows(g, n, q, full=G, last=0):
                if not is_before(g, NRING):
                    sp.wait_ge(n_res, g - (NRING - 1))
                    hold(sp, passed["sp"])
                windows = full + (last > 0)
                _, rows = nc.values_load_multi_w_load_instructions(
                    row_tab[0:1, bass.ds(g * G, windows)], (mybir.EngineType.SP,), min_val=0, max_val=ROWS - SEG,
                    skip_runtime_bounds_check_because="first_row is clamped to EP - SEG or counts compacted rows")
                for j, row in enumerate(rows):
                    sp.dma_start(seg[0:SEG_P, q, j, :, :].rearrange("p c f -> p (c f)"),
                                 msgs[bass.ds(row, SEG), :].rearrange("(p c) f -> p (c f)", c=CHUNKS)
                                 ).then_inc(n_seg[q], 16)

            sweep(sp, NGW - 1, load_windows, NRING)
            g = NGW - 1
            load_windows(g, g // NRING, g % NRING, LAST_FULL, LAST)

        @block.gpsimd
        def _(pool):
            nc.gpsimd.memset(src_all[:, :], 0).then_inc(s_clr, 1)
            nc.gpsimd.memset(dst_i[:, :], DST_PAD).then_inc(s_clr, 1)
            nc.gpsimd.memset(next_i[:, :], DST_PAD).then_inc(s_clr, 1)
            nc.gpsimd.memset(type_i[:, :], 0).then_inc(s_clr, 1)
            nc.gpsimd.memset(norm_all[:, :], 0.0).then_inc(s_clr, 1)
            nc.gpsimd.memset(w_mix[:, :], 0.0).then_inc(s_clr, 1)
            nc.gpsimd.iota(iota_i[:, :], [[1, P]], base=0, channel_multiplier=0).then_inc(s_cst, 1)
            nc.gpsimd.iota(part_i[:, :], [[0, 1]], base=0, channel_multiplier=1).then_inc(s_cst, 1)
            nc.gpsimd.iota(win_i[:, :], [[P, NGW * G]], base=0, channel_multiplier=0).then_inc(s_cst, 1)
            pool.wait_ge(s_src, 32)

            def add_pair(t, r):
                pool.wait_ge(s_z, t + 1)
                nc.gpsimd.tensor_tensor(u[:, r, :], z[:, r, 0, :], z[:, r, 1, :], ALU.add).then_inc(s_u, 1)

            def dst_column(g, n, q):
                if not is_before(g, RING):
                    pool.wait_ge(s_mst[q], n * 16)
                nc.gpsimd.tensor_copy(msg[:, q, :, F:C], dst_f[:, bass.ds(g * G, G)].unsqueeze(2)).then_inc(s_dcol, 1)

            def gathers(g, n, q):
                if not beyond(g, NG):
                    if not is_before(g, RING):
                        pool.wait_ge(s_gather[q * G + G - 1], n * 16)
                    nc.gpsimd.tensor_copy(idx[:, q, :], src_all[:, bass.ds(g * G, G)]).then_inc(s_idx, 1)
                    pool.wait_ge(s_idx, g + 1)
                    if not is_before(g, RING):
                        pool.wait_ge(s_relu, g * G - (RING - 1) * G)
                    hold(pool, passed["pool"])
                for j in range(G):
                    if not beyond(g, NG):
                        nc.gpsimd.indirect_dma_start(
                            xg[:, q, j, :], None, x, bass.IndirectOffsetOnAxis(ap=idx[:, q, j:j + 1], axis=0)
                        ).then_inc(s_gather[q * G + j], 16)
                    if not is_before(g, 3):
                        add_pair(g * G + (j - 3 * G), (q * G + j) % RING)
                if not is_before(g, 2):
                    if is_before(g, 3):
                        pool.wait_ge(s_con, 1)
                    dst_column(g - 2, round_before(n, q, 2), (q - 2) % RING)

            sweep(pool, NG, gathers)
            gathers(NG, NG // RING, NG % RING)
            gathers(NG + 1, (NG + 1) // RING, (NG + 1) % RING)
            for t in range((NG - 1) * G, NT):
                add_pair(t, t % RING)

            pool.wait_ge(s_tab, 48)
            with pool.If(pool.value_load(mode, min_val=0, max_val=1) > 0):
                pool.wait_ge(c_zst, (NW + 2) * 16)
                with pool.Fori(0, NT) as t:
                    pool.wait_ge(c_idx, t + 1)
                    hold(pool, passed["pool"])
                    nc.gpsimd.indirect_dma_start(
                        ccur[:, :], None, msgs, bass.IndirectOffsetOnAxis(ap=cidx[:, :], axis=0)).then_inc(c_cur, 16)
                    pool.wait_ge(c_new, t + 1)
                    hold(pool, passed["pool"])
                    nc.gpsimd.indirect_dma_start(
                        msgs, bass.IndirectOffsetOnAxis(ap=cidx[:, :], axis=0), ccur[:, :], None).then_inc(c_st, 16)
                    pool.wait_ge(c_st, t * 16 + 16)

            def store_results(g, q, full=G, last=0):
                pool.wait_ge(n_res, g + 1)
                hold(pool, passed["pool"])
                if full:
                    pool.dma_start(OUT_WIN[:, bass.ds(g * G, full), :], res[:, q, 0:full, :]).then_inc(n_out[q], 16)
                if last:
                    pool.dma_start(out[(NW - 1) * P:N, :], res[0:last, q, full, :]).then_inc(n_out[q], 16)

            def load_x(g, n, q, full=G, last=0):
                if not is_before(g, NRING):
                    pool.wait_ge(n_res, g - (NRING - 1))
                    hold(pool, passed["pool"])
                if full:
                    pool.dma_start(xw[:, q, 0:full, :], X_WIN[:, bass.ds(g * G, full), :]).then_inc(n_x[q], 16)
                if last:
                    pool.dma_start(xw[0:last, q, full, :], x[(NW - 1) * P:N, :]).then_inc(n_x[q], 16)
                if not is_before(g, 3):
                    store_results(g - 3, (q - 3) % NRING)

            sweep(pool, NGW - 1, load_x, NRING)
            g = NGW - 1
            load_x(g, g // NRING, g % NRING, LAST_FULL, LAST)
            store_results(g - 2, (g - 2) % NRING)
            store_results(g - 1, (g - 1) % NRING)
            store_results(g, g % NRING, LAST_FULL, LAST)
            for q in range(NRING):
                pool.wait_ge(n_out[q], 16 * (len(range(q, NGW, NRING)) + (q == g % NRING and LAST_FULL > 0)))

        @block.scalar
        def _(act):
            def scale_bases(g, q, j):
                t, r = g * G + j, (q * G + j) % RING
                if j == 0:
                    act.wait_ge(s_mix, g + 1)
                if not is_before(g, 1) or j >= RING:
                    act.wait_ge(s_a, g * (2 * G) + 2 * (j - RING + 1))
                act.wait_ge(s_y_high, t + 1)
                nc.scalar.activation(z[:, r, 2, :], y_ps[r][:, B // 2, :], ACT.Copy,
                                     scale=mix[:, q, j, B // 2:B // 2 + 1]).then_inc(s_z_high, 1)
                act.wait_ge(s_y, t + 1)
                for b in range(2):
                    ins = nc.scalar.activation(z[:, r, b, :], y_ps[r][:, b, :], ACT.Copy, scale=mix[:, q, j, b:b + 1])
                ins.then_inc(s_z, 1)

            def step(g, n, q):
                def mixing(j):
                    if not is_before(g, 1):
                        scale_bases(g - 1, (q - 1) % RING, j)

                def normalised(tiles):
                    for j in tiles:
                        nc.scalar.activation(h[:, q, j, :], xg[:, q, j, :], ACT.Relu,
                                             bias=neg_mean[:, q, j:j + 1]).then_inc(s_relu, 1)

                mixing(0)
                act.wait_ge(s_mean, g + 1)
                if not is_before(g, RING):
                    act.wait_ge(s_hT, g - (RING - 1))
                normalised(range(0, G // 2))
                if not is_before(g, RING):
                    act.wait_ge(s_small, g * 2 - (RING - 1) * 2)
                nc.scalar.activation(std[:, q, :], mv[:, q, :, 1], ACT.Sqrt, bias=eps_col[:, 0:1]).then_inc(s_std, 1)
                mixing(1)
                normalised(range(G // 2, G))
                act.wait_ge(s_hotT, g + 1)
                if not is_before(g, RING):
                    act.wait_ge(s_mix_ps, g - (RING - 1))
                nc.scalar.activation(hotT[:, q, :], mix_ps[:, 0:P], ACT.Copy).then_inc(s_hotT_sb, 1)
                mixing(2)
                act.wait_ge(s_hT, g + 1)
                if not is_before(g, RING):
                    act.wait_ge(s_y, g * G - (RING - 1) * G)
                nc.scalar.activation(hT[:, q, :, :], hT_ps[:, :, :], ACT.Copy).then_inc(s_hT_sb, 1)
                mixing(3)

            act.wait_ge(s_con, 1)
            sweep(act, NG, step)
            for j in range(G):
                scale_bases(NG - 1, (NG - 1) % RING, j)

            def window_std(g, q):
                act.wait_ge(n_mv, g + 1)
                nc.scalar.activation(nstd[:, q, :], nmv[:, q, :, 1], ACT.Sqrt, bias=eps_col[:, 0:1]).then_inc(n_std, 1)

            def node_step(g, n, q, ahead=True):
                act.wait_ge(n_shift, g + 1)
                if not is_before(g, NRING):
                    act.wait_ge(n_hT, g - (NRING - 1))
                for j in range(G):
                    ins = nc.scalar.activation(hw[:, q, j, :], xw[:, q, j, :], ACT.Relu, bias=shift[:, q, j:j + 1],
                                               scale=nrstd[:, q, j:j + 1])
                ins.then_inc(n_h, 1)
                if ahead:
                    window_std(g + 1, (q + 1) % NRING)
                act.wait_ge(n_hT, g + 1)
                if not is_before(g, NRING):
                    act.wait_ge(n_y, g - (NRING - 1))
                nc.scalar.activation(hwT[:, q, :, :], hwT_ps[q % 2], ACT.Copy).then_inc(n_hT_sb, 1)

            window_std(0, 0)
            sweep(act, NGW - 1, node_step, NRING)
            node_step(NGW - 1, (NGW - 1) // NRING, (NGW - 1) % NRING, False)

        @block.tensor
        def _(pe):
            pe.wait_ge(s_meta, 1)

            def count(t, first, last):
                return nc.tensor.matmul(mix_ps[0:HI, 256:256 + LO], hi_hot[:, t, :], lo_hot[:, t, :],
                                        start=first, stop=last)

            for t in range(NT):
                mm = count(t, t == 0, t == NT - 1)
            mm.then_inc(s_hist, 1)
            pe.wait_ge(s_meta, 2)
            nc.tensor.matmul(mix_ps[0:HI, 300:301], above[0:HI, 0:HI], upto[:, LO - 1:LO], start=True, stop=True)
            nc.tensor.matmul(mix_ps[:, 302:303], ones[:, :], bad[:, 3:4], start=True, stop=True).then_inc(s_off, 1)

            pe.wait_ge(s_wt, 16 * (3 + G))

            def products(g, q, j):
                r = (q * G + j) % RING
                if not is_before(g, 1) or j >= RING:
                    pe.wait_ge(s_a, g * (2 * G) + 2 * (j - RING + 1))
                for b0, done in ((B // 2, s_y_high), (0, s_y)):
                    nc.tensor.matmul(y_ps[r][:, b0:b0 + B // 2, :], hT[:, q, j, :],
                                     w_all[:, b0:b0 + B // 2, :], start=True, stop=True).then_inc(done, 1)

            def step(g, n, q):
                def messages(j):
                    if not is_before(g, 1):
                        if j == 0:
                            pe.wait_ge(s_hT_sb, g)
                        products(g - 1, (q - 1) % RING, j)

                messages(0)
                messages(1)
                pe.wait_ge(s_hot, g + 1)
                if not is_before(g, 1):
                    pe.wait_ge(s_mix, g)
                nc.tensor.transpose(mix_ps[:, 0:P], hot[:, q, :, :].rearrange("p t r -> p (t r)"),
                                    ident[:, :]).then_inc(s_hotT, 1)
                messages(2)
                pe.wait_ge(s_hotT_sb, g + 1)
                nc.tensor.matmul(mix_ps[:, P:P + G * B], hotT[:, q, :], w_mix[:, :],
                                 start=True, stop=True).then_inc(s_mix_ps, 1)
                pe.wait_ge(s_relu, g * G + G)
                for j in range(G):
                    mm = nc.tensor.transpose(hT_ps[:, j, :], h[:, q, j, :], ident[:, :])
                mm.then_inc(s_hT, 1)
                messages(3)

            sweep(pe, NG, step)
            pe.wait_ge(s_hT_sb, NG)
            for j in range(G):
                products(NG - 1, (NG - 1) % RING, j)

            pe.wait_ge(s_tab, 48)
            with pe.If(pe.value_load(mode, min_val=0, max_val=1) > 0):
                with pe.Fori(0, NT) as t:
                    pe.wait_ge(c_dst, t + 1)
                    nc.tensor.transpose(hT_ps[:, 0, :], cdst[:, :], ident[:, :]).then_inc(c_row, 1)
                    pe.wait_ge(c_v, t * 7 + 1)
                    nc.tensor.matmul(mix_ps[:, 0:F], ceq[:, :], cm[:, 0:F], start=True, stop=True).then_inc(c_sum, 1)

            def window_sums(g, n, q, windows=G):
                pe.wait_ge(n_hT_sb, g + 1)
                pe.wait_ge(n_pick, g + 1)
                if not is_before(g, NRING):
                    pe.wait_ge(n_res, g - (NRING - 1))
                for j in range(windows):
                    y = win_ps[q][:, j, :]
                    nc.tensor.matmul(y, hwT[:, q, j, :], w_loop[:, :], start=True, stop=False)
                    nc.tensor.matmul(y, pick[:, q, j, 0, :][0:SEG_P], seg[0:SEG_P, q, j, 0, 0:F],
                                     start=False, stop=False)
                    mm = nc.tensor.matmul(y, pick[:, q, j, 1, :][0:SEG_P + 1], seg[0:SEG_P + 1, q, j, 1, 0:F],
                                          start=False, stop=True)
                mm.then_inc(n_y, 1)

            def node_step(g, n, q):
                if not is_before(g, 1):
                    window_sums(g - 1, round_before(n, q), (q - 1) % NRING)
                pe.wait_ge(n_h, g + 1)
                if not is_before(g, 2):
                    pe.wait_ge(n_hT_sb, g - 1)
                for j in range(G):
                    mm = nc.tensor.transpose(hwT_ps[q % 2][:, j, :], hw[:, q, j, :], ident[:, :])
                mm.then_inc(n_hT, 1)

            sweep(pe, NGW, node_step, NRING)
            g = NGW - 1
            window_sums(g, g // NRING, g % NRING, LAST_FULL + 1)

        @block.vector
        def _(dve):
            nc.vector.memset(ones[:, :], 1.0)
            nc.vector.memset(eps_col[:, :], EPS)
            nc.vector.memset(bad[:, :], 0.0)
            nc.vector.memset(pick[SEG_P:P, :, :, :, :], 1.0)
            dve.wait_ge(s_cst, 3)
            nc.vector.tensor_copy(iota_n[:, :], iota_i[:, :])
            nc.vector.tensor_copy(part_f[:, :], part_i[:, :])
            nc.vector.tensor_copy(win_off[:, :], win_i[:, :]).then_inc(s_num, 1)
            dve.wait_ge(s_num, 1)
            nc.vector.tensor_scalar(ident[:, :], iota_n[:, :], part_f[:, 0:1], None, ALU.is_equal)
            nc.vector.tensor_scalar(above[:, :], iota_n[:, :], part_f[:, 0:1], None, ALU.is_gt)
            nc.vector.tensor_scalar(below[:, :], iota_n[:, :], part_f[:, 0:1], None, ALU.is_lt)
            dve.wait_ge(s_ld, 16 * 8)
            nc.vector.tensor_copy(type_f[:, :], type_i[:, :])
            nc.vector.tensor_copy(next_f[:, :], next_i[:, :])
            nc.vector.tensor_copy(dst_f[:, :], dst_i[:, :]).then_inc(s_con, 1)

            def after(ins):
                done[0] += 1
                ins.then_inc(s_num, 1)

            def settle():
                dve.wait_ge(s_num, done[0])

            done = [1]
            nc.vector.tensor_scalar(lo_i[:, :], dst_i[:, :], P.bit_length() - 1, LO - 1,
                                    ALU.logical_shift_right, ALU.bitwise_and)
            after(nc.vector.tensor_scalar(hi_i[:, :], dst_i[:, :], (P * LO).bit_length() - 1, None,
                                          ALU.logical_shift_right))
            settle()
            nc.vector.tensor_copy(lo_f[:, :], lo_i[:, :])
            after(nc.vector.tensor_copy(hi_f[:, :], hi_i[:, :]))
            settle()
            nc.vector.tensor_tensor(lo_hot[:, :, :], lo_f[:, :].unsqueeze(2).to_broadcast([P, NT, LO]),
                                    iota_n[:, 0:LO].unsqueeze(1).to_broadcast([P, NT, LO]), ALU.is_equal)
            nc.vector.tensor_tensor(hi_hot[:, :, :], hi_f[:, :].unsqueeze(2).to_broadcast([P, NT, HI]),
                                    iota_n[:, 0:HI].unsqueeze(1).to_broadcast([P, NT, HI]),
                                    ALU.is_equal).then_inc(s_meta, 1)
            dve.wait_ge(s_con, 1)
            nc.vector.tensor_tensor(falls[:, 0:NT - 1], dst_f[:, 0:NT - 1], dst_f[:, 1:NT], ALU.is_gt)
            after(nc.vector.tensor_tensor(falls[:, NT - 1:NT], dst_f[:, NT - 1:NT], next_f[:, :], ALU.is_gt))
            settle()
            after(nc.vector.tensor_reduce(bad[:, 0:1], falls[:, :], AX_X, ALU.max))
            dve.wait_ge(s_hist, 1)
            after(nc.vector.tensor_copy(hist[:, :], mix_ps[0:HI, 256:256 + LO]))
            settle()
            nc.vector.tensor_tensor_scan(upto[:, :], ones[0:HI, 0:LO], hist[:, :], 0.0, ALU.mult, ALU.add)
            after(nc.vector.tensor_scalar(big[:, :], hist[:, :], float(SEG), None, ALU.is_gt))
            settle()
            after(nc.vector.tensor_reduce(bad[0:HI, 1:2], big[:, :], AX_X, ALU.max))
            settle()
            nc.vector.tensor_tensor(bad[:, 3:4], bad[:, 0:1], bad[:, 1:2], ALU.add).then_inc(s_meta, 1)
            dve.wait_ge(s_off, 1)
            nc.vector.tensor_scalar(mode_f[:, :], mix_ps[:, 302:303], 0.5, None, ALU.is_gt)
            nc.vector.tensor_scalar(big[:, :], part_f[0:HI, 0:1].to_broadcast([HI, LO]), float(LO * P), float(EP),
                                    ALU.mult, ALU.add)
            after(nc.vector.scalar_tensor_tensor(out=start[:, :], in0=upto[:, :], scalar=mix_ps[0:HI, 300:301],
                                                 in1=hist[:, :], op0=ALU.add, op1=ALU.subtract))
            settle()
            nc.vector.tensor_scalar(start_c[:, :], start[:, :], float(EP - SEG), None, ALU.min)
            after(nc.vector.scalar_tensor_tensor(out=hist[:, :], in0=iota_n[0:HI, 0:LO], scalar=float(P),
                                                 in1=big[:, :], op0=ALU.mult, op1=ALU.add))
            settle()
            after(nc.vector.tensor_tensor(upto[:, :], hist[:, :], start_c[:, :], ALU.subtract))
            settle()
            nc.vector.tensor_copy(mode_i[:, :], mode_f[:, :])
            nc.vector.scalar_tensor_tensor(out=start_i[:, :], in0=upto[:, :], scalar=mode_f[0:HI, 0:1],
                                           in1=start_c[:, :], op0=ALU.mult, op1=ALU.add).then_inc(s_start, 1)

            def add(acc, r, c, base, first):
                return nc.vector.scalar_tensor_tensor(out=acc, in0=y_ps[r][:, base, :], scalar=c[:, base:base + 1],
                                                      in1=first, op0=ALU.mult, op1=ALU.add)

            def sum_high(g, q, j, base):
                r, before = (q * G + j) % RING, g * (3 * G) + 3 * j + (base - 5)
                if base == 5:
                    dve.wait_ge(s_z_high, g * G + j + 1)
                    first = z[:, r, 2, :]
                    if not is_before(g, 1) or j >= RING:
                        dve.wait_ge(s_msg, g * G + j - (RING - 1))
                else:
                    dve.wait_ge(s_b, before)
                    first = sum_b[:, r, :]
                add(sum_b[:, r, :], r, mix[:, q, j, :], base, first).then_inc(s_b, 1)

            def sum_low(g, q, j, base):
                r, before = (q * G + j) % RING, g * (2 * G) + 2 * j + (base - 2)
                if base == 2:
                    dve.wait_ge(s_u, g * G + j + 1)
                    first = u[:, r, :]
                else:
                    dve.wait_ge(s_b, g * (3 * G) + 3 * j + 3)
                    dve.wait_ge(s_a, before)
                    first = sum_a[:, r, :]
                add(sum_a[:, r, :], r, mix[:, q, j, :], base, first).then_inc(s_a, 1)

            def message(g, n, q, j):
                r = (q * G + j) % RING
                if j == 0 and not is_before(g, RING):
                    dve.wait_ge(s_mst[q], n * 16)
                dve.wait_ge(s_a, g * (2 * G) + 2 * j + 2)
                nc.vector.tensor_tensor(msg[:, q, j, 0:F], sum_a[:, r, :], sum_b[:, r, :], ALU.add).then_inc(s_msg, 1)

            def tile_slot(g, n, q, j, more):
                now = not is_before(g, 1) and not beyond(g, NG + 1)
                p = g - 1, round_before(n, q), (q - 1) % RING
                b = p if j else (g - 2, round_before(n, q, 2), (q - 2) % RING)
                bj = (j - 1) % G
                past = not is_before(g, 1 if j else 2)
                an, aq = round_after(n, q), (q + 1) % RING
                if now:
                    sum_high(p[0], p[2], j, 5)
                if past:
                    sum_low(b[0], b[2], bj, 2)
                if now:
                    sum_high(p[0], p[2], j, 6)
                if past:
                    sum_low(b[0], b[2], bj, 3)
                if more:
                    dve.wait_ge(s_gather[aq * G + j], an * 16 + 16)
                    if j == 0 and not is_before(g, RING - 1):
                        dve.wait_ge(s_bn, g * (2 * G) - (RING - 2) * (2 * G))
                        dve.wait_ge(s_std, g - (RING - 2))
                        dve.wait_ge(s_relu, g * G - (RING - 2) * G)
                    nc.vector.bn_stats(stats[:, aq, j, :], xg[:, aq, j, :]).then_inc(s_bn, 1)
                if now:
                    sum_high(p[0], p[2], j, 7)
                if more:
                    dve.wait_ge(s_bn, g * (2 * G) + (2 * G + 2 * j + 1))
                if past:
                    message(*b, bj)
                elif more:
                    hold(dve, passed["dve"])
                if more:
                    nc.vector.bn_aggr(mv[:, aq, j, :], stats[:, aq, j, :]).then_inc(s_bn, 1)

            def one_hot(g, q):
                if not is_before(g, RING):
                    dve.wait_ge(s_hotT, g - (RING - 1))
                nc.vector.tensor_tensor(hot[:, q, :, :],
                                        type_f[:, bass.ds(g * G, G)].unsqueeze(2).to_broadcast([P, G, R]),
                                        iota_n[:, 0:R].unsqueeze(1).to_broadcast([P, G, R]),
                                        ALU.is_equal).then_inc(s_hot, 1)

            def means(g, q):
                dve.wait_ge(s_bn, g * (2 * G) + 2 * G)
                nc.vector.tensor_scalar(neg_mean[:, q, :], mv[:, q, :, 0], -1.0, None, ALU.mult).then_inc(s_mean, 1)

            def step(g, n, q):
                more, here = not beyond(g, NG - 1), not beyond(g, NG)
                tile_slot(g, n, q, 0, more)
                tile_slot(g, n, q, 1, more)
                if here:
                    dve.wait_ge(s_std, g + 1)
                    nc.vector.reciprocal(rstd[:, q, :], std[:, q, :]).then_inc(s_small, 1)
                tile_slot(g, n, q, 2, more)
                if here:
                    dve.wait_ge(s_small, g * 2 + 1)
                    nc.vector.tensor_tensor(gain[:, q, :], rstd[:, q, :], norm_all[:, bass.ds(g * G, G)],
                                            ALU.mult).then_inc(s_small, 1)
                    dve.wait_ge(s_small, g * 2 + 2)
                    dve.wait_ge(s_mix_ps, g + 1)
                    nc.vector.tensor_tensor(mix[:, q, :, :],
                                            mix_ps[:, P:P + G * B].rearrange("p (t b) -> p t b", t=G),
                                            gain[:, q, :].unsqueeze(2).to_broadcast([P, G, B]),
                                            ALU.mult).then_inc(s_mix, 1)
                tile_slot(g, n, q, 3, more)
                if more:
                    one_hot(g + 1, (q + 1) % RING)
                    means(g + 1, (q + 1) % RING)

            for j in range(G):
                dve.wait_ge(s_gather[j], 16)
                nc.vector.bn_stats(stats[:, 0, j, :], xg[:, 0, j, :]).then_inc(s_bn, 1)
                dve.wait_ge(s_bn, 2 * j + 1)
                nc.vector.bn_aggr(mv[:, 0, j, :], stats[:, 0, j, :]).then_inc(s_bn, 1)
            one_hot(0, 0)
            means(0, 0)
            sweep(dve, NG - 1, step)
            step(NG - 1, (NG - 1) // RING, (NG - 1) % RING)
            step(NG, NG // RING, NG % RING)
            last = NG - 1, (NG - 1) // RING, (NG - 1) % RING
            sum_low(last[0], last[2], G - 1, 2)
            sum_low(last[0], last[2], G - 1, 3)
            message(*last, G - 1)

            dve.wait_ge(s_tab, 48)
            with dve.If(dve.value_load(mode, min_val=0, max_val=1) > 0):
                nc.vector.memset(cz[:, 0:F], 0.0)
                nc.vector.tensor_scalar(cz[:, F:C], part_f[:, :], -float(P), None, ALU.add).then_inc(c_own, 1)
                with dve.Fori(0, NW + 2) as w:
                    dve.wait_ge(c_own, w + 1)
                    nc.vector.tensor_scalar(cz[:, F:C], cz[:, F:C], float(P), None, ALU.add).then_inc(c_own, 1)
                    dve.wait_ge(c_own, w + 2)
                    nc.vector.tensor_copy(cc[:, 7:8], cz[:, F:C]).then_inc(c_zero, 1)
                    dve.wait_ge(c_zst, w * 16 + 16)
                    hold(dve, passed["dve"])
                with dve.Fori(0, NT) as t:
                    tile_dst = cm[:, F:C]
                    dve.wait_ge(c_ld, t * 16 + 16)
                    nc.vector.tensor_scalar(cdst[:, :], ones[:, :], tile_dst, None, ALU.mult).then_inc(c_dst, 1)
                    dve.wait_ge(c_row, t + 1)
                    nc.vector.tensor_scalar(ceq[:, :], hT_ps[:, 0, :], tile_dst, None, ALU.is_equal).then_inc(c_v, 1)
                    nc.vector.tensor_scalar(cc[:, 1:2], tile_dst, N - 0.5, None, ALU.is_gt).then_inc(c_v, 1)
                    nc.vector.scalar_tensor_tensor(out=cc[:, 3:4], in0=part_f[:, :], scalar=float(DUMMY - EP),
                                                   in1=tile_dst, op0=ALU.add, op1=ALU.subtract).then_inc(c_v, 1)
                    dve.wait_ge(c_v, t * 7 + 3)
                    nc.vector.tensor_tensor(cwork[:, :], ceq[:, :], below[:, :], ALU.mult).then_inc(c_v, 1)
                    dve.wait_ge(c_v, t * 7 + 4)
                    nc.vector.tensor_reduce(cc[:, 0:1], cwork[:, :], AX_X, ALU.add).then_inc(c_v, 1)
                    dve.wait_ge(c_v, t * 7 + 5)
                    nc.vector.scalar_tensor_tensor(out=cc[:, 2:3], in0=cc[:, 0:1], scalar=1.0, in1=cc[:, 1:2],
                                                   op0=ALU.min, op1=ALU.max).then_inc(c_v, 1)
                    dve.wait_ge(c_v, t * 7 + 6)
                    nc.vector.tensor_tensor(cc[:, 4:5], cc[:, 2:3], cc[:, 3:4], ALU.mult).then_inc(c_v, 1)
                    dve.wait_ge(c_v, t * 7 + 7)
                    nc.vector.scalar_tensor_tensor(out=cidx[:, :], in0=tile_dst, scalar=float(EP), in1=cc[:, 4:5],
                                                   op0=ALU.add, op1=ALU.add).then_inc(c_idx, 1)
                    dve.wait_ge(c_cur, t * 16 + 16)
                    dve.wait_ge(c_sum, t + 1)
                    nc.vector.tensor_tensor(ccur[:, 0:F], ccur[:, 0:F], mix_ps[:, 0:F], ALU.add).then_inc(c_new, 1)

            def window_stats(g, n, q, x_loads=1):
                dve.wait_ge(n_x[q], n * 16 + 16 * x_loads)
                for j in range(G):
                    ins = nc.vector.bn_stats(nstats[:, q, j, :], xw[:, q, j, :])
                ins.then_inc(n_bn, 1)
                dve.wait_ge(n_bn, g + 1)
                hold(dve, passed["dve"])
                for j in range(G):
                    ins = nc.vector.bn_aggr(nmv[:, q, j, :], nstats[:, q, j, :])
                ins.then_inc(n_mv, 1)

            def window_rows(g, n, q, windows=G):
                dve.wait_ge(n_seg[q], n * (16 * G) + 16 * windows)
                nc.vector.tensor_tensor(rel[:, q, 0:windows, :], seg[0:SEG_P, q, 0:windows, :, F],
                                        win_off[0:SEG_P, bass.ds(g * G, windows)].unsqueeze(2).to_broadcast(
                                            [SEG_P, windows, CHUNKS]), ALU.subtract).then_inc(n_rel, 1)
                if not is_before(g, NRING):
                    dve.wait_ge(n_y, g - (NRING - 1))
                dve.wait_ge(n_rel, g + 1)
                shape = [SEG_P, windows * CHUNKS, P]
                nc.vector.tensor_tensor(
                    pick[0:SEG_P, q, 0:windows, :, :].rearrange("p j c n -> p (j c) n"),
                    iota_n[0:SEG_P, :].unsqueeze(1).to_broadcast(shape),
                    rel[:, q, 0:windows, :].rearrange("p j c -> p (j c)").unsqueeze(2).to_broadcast(shape),
                    ALU.is_equal).then_inc(n_pick, 1)

            def window_shift(g, q):
                dve.wait_ge(n_std, g + 1)
                nc.vector.reciprocal(nrstd[:, q, :], nstd[:, q, :]).then_inc(n_rstd, 1)
                dve.wait_ge(n_rstd, g + 1)
                nc.vector.scalar_tensor_tensor(out=shift[:, q, :], in0=nmv[:, q, :, 0], scalar=-1.0,
                                               in1=nrstd[:, q, :], op0=ALU.mult, op1=ALU.mult).then_inc(n_shift, 1)

            def results(g, n, q, windows=G):
                dve.wait_ge(n_y, g + 1)
                if not is_before(g, NRING):
                    dve.wait_ge(n_out[q], n * 16)
                nc.vector.scalar_tensor_tensor(out=res[:, q, 0:windows, :], in0=win_ps[q][:, 0:windows, :], scalar=0.0,
                                               in1=xw[:, q, 0:windows, :], op0=ALU.max,
                                               op1=ALU.add).then_inc(n_res, 1)

            def node_step(g, n, q, windows=G, x_loads=1):
                window_shift(g, q)
                ahead = g + 1, n if q < NRING - 1 else n + 1, (q + 1) % NRING
                window_stats(*ahead, x_loads)
                window_rows(*ahead, windows)
                if not is_before(g, 1):
                    results(g - 1, round_before(n, q), (q - 1) % NRING)

            window_stats(0, 0, 0)
            window_rows(0, 0, 0)
            sweep(dve, NGW - 2, node_step, NRING)
            g = NGW - 2
            node_step(g, g // NRING, g % NRING, LAST_FULL + 1, 1 + (LAST_FULL > 0))
            g = NGW - 1
            window_shift(g, g % NRING)
            results(g - 1, (g - 1) // NRING, (g - 1) % NRING)
            results(g, g // NRING, g % NRING, LAST_FULL + 1)


_INS = ["x", "src", "dst", "edge_type_32", "edge_weight1", "L0_gnn_weight", "L0_gnn_w_comp", "L0_gnn_loop_weight",
        "L0_gnn_h_bias"]


def kernel(**inputs):
    import concourse.bacc as bacc
    from concourse.bass_utils import run_bass_kernel_spmd

    nc = bacc.Bacc("TRN2", target_bir_lowering=False, num_devices=1)
    arrays, args = {}, []
    for name in _INS:
        a = np.ascontiguousarray(inputs[name])
        arrays[name] = a
        args.append(nc.dram_tensor(name, a.shape, mybir.dt.from_np(a.dtype), kind="ExternalInput").ap())
    args.append(nc.dram_tensor("out", inputs["x"].shape, F32, kind="ExternalOutput").ap())
    build_layer(nc, *args)
    r = run_bass_kernel_spmd(nc, [arrays], core_ids=[0])
    return r.results[0]["out"]
```

```python
from contextlib import ExitStack

import numpy as np

import concourse.bass as bass
from concourse import mybir

ALU = mybir.AluOpType
ACT = mybir.ActivationFunctionType
F32 = mybir.dt.float32
BF16 = mybir.dt.bfloat16
I32 = mybir.dt.int32
AX_X = mybir.AxisListType.X

P = 128
G = 4
RING = 3
EPS = 1e-5
CHUNKS = 2
DV = 2
NRING = 4
LRING = 8
SEG_P = 96


def sweep(eng, count, step, ring=RING, peel=5):
    for g in range(min(peel, count)):
        step(g, g // ring, g % ring)
    rounds = max(0, (count - peel) // ring)
    if rounds:
        with eng.Fori(0, rounds) as i:
            for k in range(peel, peel + ring):
                step(i * ring + k, i + k // ring, k % ring)
    for g in range(peel + ring * rounds, count):
        step(g, g // ring, g % ring)


def hold(eng, passed):
    eng.sem_inc(passed, 1)


def round_before(n, q, k=1, ring=RING):
    return n + (q - k) // ring


def round_after(n, q, ring=RING):
    return n + (q + 1) // ring


def beyond(g, n):
    return isinstance(g, int) and g >= n


def is_before(g, n):
    return isinstance(g, int) and g < n


def build_layer(nc, x, src, dst, etype, norm, weight, w_comp, loop_weight, bias, out):
    N, D = x.shape
    E = src.shape[0]
    R, B = w_comp.shape
    F = loop_weight.shape[1]
    NT = -(-E // P)
    NT = -(-NT // G) * G
    NG = NT // G
    EP = NT * P
    FULL_P, REST = E // NT, E % NT
    NW = -(-N // P)
    LAST = N - (NW - 1) * P
    NGW = -(-NW // G)
    SEG = SEG_P * CHUNKS
    LO = 32
    HI = -(-(NW + 1) // LO)
    DST_PAD = HI * LO * P - 1
    NODE_ROWS = (NW + 1) * P
    DUMMY = EP + NODE_ROWS
    ROWS = DUMMY + P
    C = F + 1
    assert D == P and F == P and R * G == P and 2 * G * P <= 1024 and B == 8
    assert REST > 0 and EP - E <= SEG and NG > RING and NGW > LRING and LRING % NRING == 0

    msgs = nc.dram_tensor("msgs", [ROWS, C], F32, kind="Internal").ap()
    first_row = nc.dram_tensor("first_row", [HI * LO, 1], I32, kind="Internal").ap()
    mode = nc.dram_tensor("mode", [1, 1], I32, kind="Internal").ap()

    ctx = ExitStack()
    with ctx:
        def sb(name, shape, dt=F32):
            return ctx.enter_context(nc.sbuf_tensor(name, shape, dt))

        def psum(name, shape, dt=F32):
            return ctx.enter_context(nc.psum_tensor(name, shape, dt))

        def sem(name):
            return ctx.enter_context(nc.semaphore(name))

        iota_i = sb("iota_i", [P, P], I32)
        part_i = sb("part_i", [P, 1], I32)
        iota_n = sb("iota_n", [P, P])
        part_f = sb("part_f", [P, 1])
        ident = sb("ident", [P, P])
        above = sb("above", [P, P])
        below = sb("below", [P, P])
        ones = sb("ones", [P, P])
        eps_col = sb("eps_col", [P, 1])
        win_i = sb("win_i", [P, NGW * G], I32)
        win_off = sb("win_off", [P, NGW * G])
        w_all = sb("w_all", [P, B, F])
        w_loop = sb("w_loop", [P, F])
        w_mix = sb("w_mix", [P, G * B])
        src_all = sb("src_all", [P, NT], I32)
        type_i = sb("type_i", [P, NT], I32)
        type_f = sb("type_f", [P, NT])
        norm_all = sb("norm_all", [P, NT])
        dst_i = sb("dst_i", [P, NT], I32)
        dst_f = sb("dst_f", [P, NT])
        next_i = sb("next_i", [P, 1], I32)
        next_f = sb("next_f", [P, 1])
        hi_i = sb("hi_i", [P, NT], I32)
        lo_i = sb("lo_i", [P, NT], I32)
        hi_b = sb("hi_b", [P, NT], BF16)
        lo_b = sb("lo_b", [P, NT], BF16)
        hi_hot = sb("hi_hot", [P, HI, NT], BF16)
        lo_hot = sb("lo_hot", [P, LO, NT], BF16)
        falls = sb("falls", [P, NT])
        bad = sb("bad", [P, 4])
        hist = sb("hist", [HI, LO])
        upto = sb("upto", [HI, LO])
        start = sb("start", [HI, LO])
        start_c = sb("start_c", [HI, LO])
        start_i = sb("start_i", [HI, LO], I32)
        before = sb("before", [HI, 1])
        big = sb("big", [HI, LO])
        row_tab = sb("row_tab", [1, HI * LO], I32)
        mode_f = sb("mode_f", [P, 1])
        mode_i = sb("mode_i", [P, 1], I32)
        xg = sb("xg", [P, RING, G, D])
        stats = sb("stats", [P, RING, DV, 6])
        mv = sb("mv", [P, RING, DV, 2])
        squares = sb("squares", [P, RING, G - DV])
        neg_mean = sb("neg_mean", [P, RING, G])
        std = sb("std", [P, RING, G])
        h = sb("h", [P, RING, G, D])
        hT = sb("hT", [P, RING, G, P])
        idx = sb("idx", [P, RING, G], I32)
        hot = sb("hot", [P, RING, G, R])
        hotT = sb("hotT", [P, RING, P])
        rstd = sb("rstd", [P, RING, G])
        gain = sb("gain", [P, RING, G])
        mix = sb("mix", [P, RING, G, B])
        z = sb("z", [P, RING, 3, F])
        u = sb("u", [P, RING, F])
        sum_a = sb("sum_a", [P, RING, F])
        sum_b = sb("sum_b", [P, RING, F])
        msg = sb("msg", [P, RING, G, C])
        xw = sb("xw", [P, LRING, G, D])
        nstats = sb("nstats", [P, NRING, G, 6])
        nmv = sb("nmv", [P, NRING, G, 2])
        nstd = sb("nstd", [P, NRING, G])
        nrstd = sb("nrstd", [P, NRING, G])
        shift = sb("shift", [P, NRING, G])
        hw = sb("hw", [P, NRING, G, D])
        hwT = sb("hwT", [P, NRING, G, P])
        seg = sb("seg", [P, LRING, G, CHUNKS, C])
        rel = sb("rel", [SEG_P, NRING, G, CHUNKS])
        pick = sb("pick", [P, NRING, G, CHUNKS, P])
        res = sb("res", [P, NRING, G, F])
        cz = sb("cz", [P, C])
        cm = sb("cm", [P, C])
        ccur = sb("ccur", [P, C])
        cdst = sb("cdst", [P, P])
        ceq = sb("ceq", [P, P])
        cwork = sb("cwork", [P, P])
        cc = sb("cc", [P, 8])
        cidx = sb("cidx", [P, 1], I32)

        y_ps = [psum(f"y_ps{r}", [P, B, F]) for r in range(RING)]
        hT_ps = psum("hT_ps", [P, G, P])
        mix_ps = psum("mix_ps", [P, 512])

        win_ps = [y_ps[0][:, 0:G, :], y_ps[1][:, 0:G, :], y_ps[2][:, 0:G, :], y_ps[0][:, G:2 * G, :]]
        hwT_ps = [hT_ps[:, :, :], mix_ps[:, :].rearrange("p (t e) -> p t e", t=G)]

        s_cst = sem("s_cst")
        passed = {e: sem(f"passed_{e}") for e in ("sp", "pool", "dve")}
        s_clr = sem("s_clr")
        s_num = sem("s_num")
        s_src = sem("s_src")
        s_ld = sem("s_ld")
        s_wt = sem("s_wt")
        s_con = sem("s_con")
        s_meta = sem("s_meta")
        s_hist = sem("s_hist")
        s_start = sem("s_start")
        s_off = sem("s_off")
        s_tab = sem("s_tab")
        s_idx = sem("s_idx")
        s_gather = [sem(f"s_gather{i}") for i in range(RING * G)]
        s_bn = sem("s_bn")
        s_mean = sem("s_mean")
        s_mean_act = sem("s_mean_act")
        s_squares = sem("s_squares")
        s_hot = sem("s_hot")
        s_std = sem("s_std")
        s_rstd = sem("s_rstd")
        s_gain = sem("s_gain")
        s_mix = sem("s_mix")
        s_relu = sem("s_relu")
        s_hotT = sem("s_hotT")
        s_hotT_sb = sem("s_hotT_sb")
        s_mix_ps = sem("s_mix_ps")
        s_hT = sem("s_hT")
        s_hT_sb = sem("s_hT_sb")
        s_y_high = sem("s_y_high")
        s_y = sem("s_y")
        s_z_high = sem("s_z_high")
        s_z = sem("s_z")
        s_u = sem("s_u")
        s_a = sem("s_a")
        s_b = sem("s_b")
        s_msg = sem("s_msg")
        s_dcol = sem("s_dcol")
        s_mst = [sem(f"s_mst{q}") for q in range(RING)]
        c_zero = sem("c_zero")
        c_zst = sem("c_zst")
        c_ld = sem("c_ld")
        c_dst = sem("c_dst")
        c_row = sem("c_row")
        c_v = sem("c_v")
        c_sum = sem("c_sum")
        c_idx = sem("c_idx")
        c_cur = sem("c_cur")
        c_new = sem("c_new")
        c_own = sem("c_own")
        c_st = sem("c_st")
        n_x = [sem(f"n_x{q}") for q in range(LRING)]
        n_seg = [sem(f"n_seg{q}") for q in range(LRING)]
        n_bn = sem("n_bn")
        n_mv = sem("n_mv")
        n_std = sem("n_std")
        n_rstd = sem("n_rstd")
        n_shift = sem("n_shift")
        n_h = sem("n_h")
        n_pick = sem("n_pick")
        n_rel = sem("n_rel")
        n_hT = sem("n_hT")
        n_hT_sb = sem("n_hT_sb")
        n_y = sem("n_y")
        n_res = sem("n_res")
        n_out = [sem(f"n_out{q}") for q in range(NRING)]

        def edges(a):
            return (a[0:FULL_P * NT].rearrange("(p t) -> p t", t=NT),
                    a[FULL_P * NT:E].rearrange("(p t) -> p t", p=1))

        def load_edges(eng, tile, a, s):
            full, rest = edges(a)
            eng.dma_start(tile[0:FULL_P, :], full).then_inc(s, 16)
            eng.dma_start(tile[FULL_P:FULL_P + 1, 0:REST], rest).then_inc(s, 16)

        msg_rows = msgs[0:EP, :].rearrange("(p t) c -> p (t c)", t=NT)
        start_flat = first_row.rearrange("(a b) c -> a (b c)", b=LO)
        X_WIN = x[0:(NW - 1) * P, :].rearrange("(w p) d -> p w d", p=P)
        OUT_WIN = out[0:(NW - 1) * P, :].rearrange("(w p) d -> p w d", p=P)
        LAST_FULL = NW - 1 - (NGW - 1) * G

        block = ctx.enter_context(nc.Block())

        @block.sync
        def _(sp):
            sp.wait_ge(s_clr, 1)
            load_edges(sp, src_all, src, s_src)
            sp.wait_ge(s_clr, 6)
            load_edges(sp, dst_i, dst, s_ld)
            sp.dma_start(next_i[0:FULL_P - 1, :],
                         dst[NT:FULL_P * NT].rearrange("(p t) -> p t", t=NT)[:, 0:1],
                         allow_slow_non_contiguous=True).then_inc(s_ld, 16)
            sp.dma_start(next_i[FULL_P - 1:FULL_P, :],
                         dst[FULL_P * NT:FULL_P * NT + 1].rearrange("(p t) -> p t", p=1)).then_inc(s_ld, 16)
            load_edges(sp, type_i, etype, s_ld)
            load_edges(sp, norm_all, norm.rearrange("e o -> (e o)"), s_ld)
            sp.dma_start(w_all[:, :, :], weight.rearrange("b d f -> d b f")).then_inc(s_wt, 16)
            sp.dma_start(w_loop[:, :], loop_weight).then_inc(s_wt, 16)
            for j in range(G):
                sp.dma_start(w_mix[R * j:R * j + R, B * j:B * j + B], w_comp).then_inc(s_wt, 16)
            sp.dma_start(seg[SEG_P:SEG_P + 1, :, :, CHUNKS - 1, 0:F].rearrange("p q j f -> p (q j) f"),
                         bias.rearrange("(a b f) -> a b f", a=1, b=1).to_broadcast([1, LRING * G, F])).then_inc(s_wt, 16)

            def store_messages(g, n, q):
                sp.wait_ge(s_msg, g * G + G)
                hold(sp, passed["sp"])
                sp.wait_ge(s_dcol, g + 1)
                hold(sp, passed["sp"])
                sp.dma_start(msg_rows[:, bass.ds(g * (G * C), G * C)],
                             msg[:, q, :, :].rearrange("p t c -> p (t c)")).then_inc(s_mst[q], 16)

            sweep(sp, NG - 3, store_messages)
            sp.wait_ge(s_start, 1)
            sp.dma_start(start_flat, start_i[:, :]).then_inc(s_tab, 16)
            sp.dma_start(mode, mode_i[0:1, :]).then_inc(s_tab, 16)
            sp.wait_ge(s_tab, 32)
            sp.dma_start(row_tab[:, :], first_row.rearrange("w c -> c w")).then_inc(s_tab, 16)
            for g in range(NG - 3, NG):
                store_messages(g, g // RING, g % RING)
            for q in range(RING):
                sp.wait_ge(s_mst[q], 16 * len(range(q, NG, RING)))

            sp.wait_ge(s_tab, 48)
            with sp.If(sp.value_load(mode, min_val=0, max_val=1) > 0):
                with sp.Fori(0, NW + 2) as w:
                    sp.wait_ge(c_zero, w + 1)
                    hold(sp, passed["sp"])
                    sp.dma_start(msgs[bass.ds(w * P + EP, P), :], cz[:, :]).then_inc(c_zst, 16)
                with sp.Fori(0, NT) as t:
                    sp.dma_start(cm[:, :], msgs[bass.ds(t * P, P), :]).then_inc(c_ld, 16)
                    sp.wait_ge(c_st, t * 16 + 16)
                    hold(sp, passed["sp"])

            def load_windows(g, n, q, full=G, last=0):
                if not is_before(g, LRING):
                    sp.wait_ge(n_res, g - (LRING - 1))
                    hold(sp, passed["sp"])
                windows = full + (last > 0)
                _, rows = nc.values_load_multi_w_load_instructions(
                    row_tab[0:1, bass.ds(g * G, windows)], (mybir.EngineType.SP,), min_val=0, max_val=ROWS - SEG,
                    skip_runtime_bounds_check_because="first_row is clamped to EP - SEG or counts compacted rows")
                for j, row in enumerate(rows):
                    sp.dma_start(seg[0:SEG_P, q, j, :, :].rearrange("p c f -> p (c f)"),
                                 msgs[bass.ds(row, SEG), :].rearrange("(p c) f -> p (c f)", c=CHUNKS)
                                 ).then_inc(n_seg[q], 16)

            sweep(sp, NGW - 1, load_windows, LRING, LRING)
            g = NGW - 1
            load_windows(g, g // LRING, g % LRING, LAST_FULL, LAST)

        @block.gpsimd
        def _(pool):
            nc.gpsimd.memset(src_all[:, :], 0).then_inc(s_clr, 1)
            nc.gpsimd.memset(dst_i[:, :], DST_PAD).then_inc(s_clr, 1)
            nc.gpsimd.memset(next_i[:, :], DST_PAD).then_inc(s_clr, 1)
            nc.gpsimd.memset(type_i[:, :], 0).then_inc(s_clr, 1)
            nc.gpsimd.memset(norm_all[:, :], 0.0).then_inc(s_clr, 1)
            nc.gpsimd.memset(w_mix[:, :], 0.0).then_inc(s_clr, 1)
            nc.gpsimd.iota(iota_i[:, :], [[1, P]], base=0, channel_multiplier=0).then_inc(s_cst, 1)
            nc.gpsimd.iota(part_i[:, :], [[0, 1]], base=0, channel_multiplier=1).then_inc(s_cst, 1)
            nc.gpsimd.iota(win_i[:, :], [[P, NGW * G]], base=0, channel_multiplier=0).then_inc(s_cst, 1)
            pool.wait_ge(s_src, 32)

            def add_pair(t, r):
                pool.wait_ge(s_z, t + 1)
                nc.gpsimd.tensor_tensor(u[:, r, :], z[:, r, 0, :], z[:, r, 1, :], ALU.add).then_inc(s_u, 1)

            def dst_column(g, n, q):
                if not is_before(g, RING):
                    pool.wait_ge(s_mst[q], n * 16)
                nc.gpsimd.tensor_copy(msg[:, q, :, F:C], dst_f[:, bass.ds(g * G, G)].unsqueeze(2)).then_inc(s_dcol, 1)

            def gains(g, q):
                pool.wait_ge(s_rstd, g + 1)
                if not is_before(g, RING):
                    pool.wait_ge(s_mix, g - (RING - 1))
                nc.gpsimd.tensor_tensor(gain[:, q, :], norm_all[:, bass.ds(g * G, G)], rstd[:, q, :],
                                        ALU.mult).then_inc(s_gain, 1)

            def gathers(g, n, q):
                if not beyond(g, NG):
                    if not is_before(g, RING):
                        pool.wait_ge(s_gather[q * G + G - 1], n * 16)
                    nc.gpsimd.tensor_copy(idx[:, q, :], src_all[:, bass.ds(g * G, G)]).then_inc(s_idx, 1)
                    pool.wait_ge(s_idx, g + 1)
                    if not is_before(g, RING):
                        pool.wait_ge(s_relu, g * G - (RING - 1) * G)
                    hold(pool, passed["pool"])
                for j in range(G):
                    if not beyond(g, NG):
                        nc.gpsimd.indirect_dma_start(
                            xg[:, q, j, :], None, x, bass.IndirectOffsetOnAxis(ap=idx[:, q, j:j + 1], axis=0)
                        ).then_inc(s_gather[q * G + j], 16)
                    if j == 2 and not is_before(g, 2):
                        gains(g - 2, (q - 2) % RING)
                    if not is_before(g, 3):
                        add_pair(g * G + (j - 3 * G), (q * G + j) % RING)
                if not is_before(g, 2):
                    if is_before(g, 3):
                        pool.wait_ge(s_con, 1)
                    dst_column(g - 2, round_before(n, q, 2), (q - 2) % RING)

            sweep(pool, NG, gathers)
            gathers(NG, NG // RING, NG % RING)
            gathers(NG + 1, (NG + 1) // RING, (NG + 1) % RING)
            for t in range((NG - 1) * G, NT):
                add_pair(t, t % RING)

            pool.wait_ge(s_tab, 48)
            with pool.If(pool.value_load(mode, min_val=0, max_val=1) > 0):
                pool.wait_ge(c_zst, (NW + 2) * 16)
                with pool.Fori(0, NT) as t:
                    pool.wait_ge(c_idx, t + 1)
                    hold(pool, passed["pool"])
                    nc.gpsimd.indirect_dma_start(
                        ccur[:, :], None, msgs, bass.IndirectOffsetOnAxis(ap=cidx[:, :], axis=0)).then_inc(c_cur, 16)
                    pool.wait_ge(c_new, t + 1)
                    hold(pool, passed["pool"])
                    nc.gpsimd.indirect_dma_start(
                        msgs, bass.IndirectOffsetOnAxis(ap=cidx[:, :], axis=0), ccur[:, :], None).then_inc(c_st, 16)
                    pool.wait_ge(c_st, t * 16 + 16)

            def store_results(g, q, full=G, last=0):
                r = q % NRING
                pool.wait_ge(n_res, g + 1)
                hold(pool, passed["pool"])
                if full:
                    pool.dma_start(OUT_WIN[:, bass.ds(g * G, full), :], res[:, r, 0:full, :]).then_inc(n_out[r], 16)
                if last:
                    pool.dma_start(out[(NW - 1) * P:N, :], res[0:last, r, full, :]).then_inc(n_out[r], 16)

            def load_x(g, n, q, full=G, last=0):
                if not is_before(g, LRING):
                    store_results(g - LRING, q)
                if full:
                    pool.dma_start(xw[:, q, 0:full, :], X_WIN[:, bass.ds(g * G, full), :]).then_inc(n_x[q], 16)
                if last:
                    pool.dma_start(xw[0:last, q, full, :], x[(NW - 1) * P:N, :]).then_inc(n_x[q], 16)

            sweep(pool, NGW - 1, load_x, LRING, LRING)
            last_g = NGW - 1
            load_x(last_g, last_g // LRING, last_g % LRING, LAST_FULL, LAST)
            for g in range(NGW - LRING, last_g):
                store_results(g, g % NRING)
            store_results(last_g, last_g % NRING, LAST_FULL, LAST)
            for r in range(NRING):
                pool.wait_ge(n_out[r], 16 * (len(range(r, NGW, NRING)) + (r == last_g % NRING and LAST_FULL > 0)))

        @block.scalar
        def _(act):
            def scale_bases(g, q, j):
                t, r = g * G + j, (q * G + j) % RING
                if j == 0:
                    act.wait_ge(s_mix, g + 1)
                if not is_before(g, 1) or j >= RING:
                    act.wait_ge(s_a, g * (2 * G) + 2 * (j - RING + 1))
                act.wait_ge(s_y_high, t + 1)
                nc.scalar.activation(z[:, r, 2, :], y_ps[r][:, B // 2, :], ACT.Copy,
                                     scale=mix[:, q, j, B // 2:B // 2 + 1]).then_inc(s_z_high, 1)
                act.wait_ge(s_y, t + 1)
                for b in range(2):
                    ins = nc.scalar.activation(z[:, r, b, :], y_ps[r][:, b, :], ACT.Copy, scale=mix[:, q, j, b:b + 1])
                ins.then_inc(s_z, 1)

            def group_means(g, n, q):
                if not is_before(g, RING):
                    act.wait_ge(s_hT, g - (RING - 1))
                    act.wait_ge(s_std, g - (RING - 1))
                    act.wait_ge(s_relu, g * G - (RING - 1) * G)
                for j in range(DV, G):
                    act.wait_ge(s_gather[q * G + j], n * 16 + 16)
                    nc.scalar.activation(h[:, q, j, :], xg[:, q, j, :], ACT.Copy, scale=-1.0 / D,
                                         accum_out=neg_mean[:, q, j:j + 1]).then_inc(s_mean_act, 1)

            def group_squares(g, q):
                for j in range(DV, G):
                    act.wait_ge(s_mean_act, g * (G - DV) + (j - DV + 1))
                    nc.scalar.activation(h[:, q, j, :], xg[:, q, j, :], ACT.Square, bias=neg_mean[:, q, j:j + 1],
                                         accum_out=squares[:, q, j - DV:j - DV + 1]).then_inc(s_squares, 1)

            def step(g, n, q):
                def mixing(j):
                    if not is_before(g, 1):
                        scale_bases(g - 1, (q - 1) % RING, j)

                def normalised(tiles):
                    for j in tiles:
                        nc.scalar.activation(h[:, q, j, :], xg[:, q, j, :], ACT.Relu,
                                             bias=neg_mean[:, q, j:j + 1]).then_inc(s_relu, 1)

                mixing(0)
                act.wait_ge(s_mean, g + 1)
                act.wait_ge(s_squares, (g + 1) * (G - DV))
                if not is_before(g, RING):
                    act.wait_ge(s_hT, g - (RING - 1))
                normalised(range(0, G // 2))
                if not is_before(g, RING):
                    act.wait_ge(s_rstd, g - (RING - 1))
                nc.scalar.activation(std[:, q, 0:DV], mv[:, q, :, 1], ACT.Sqrt, bias=eps_col[:, 0:1])
                nc.scalar.activation(std[:, q, DV:G], squares[:, q, :], ACT.Sqrt, bias=eps_col[:, 0:1],
                                     scale=1.0 / D).then_inc(s_std, 1)
                mixing(1)
                normalised(range(G // 2, G))
                act.wait_ge(s_hotT, g + 1)
                if not is_before(g, RING):
                    act.wait_ge(s_mix_ps, g - (RING - 1))
                nc.scalar.activation(hotT[:, q, :], mix_ps[:, 0:P], ACT.Copy).then_inc(s_hotT_sb, 1)
                mixing(2)
                act.wait_ge(s_hT, g + 1)
                if not is_before(g, RING):
                    act.wait_ge(s_y, g * G - (RING - 1) * G)
                nc.scalar.activation(hT[:, q, :, :], hT_ps[:, :, :], ACT.Copy).then_inc(s_hT_sb, 1)
                if not beyond(g, NG - 1):
                    group_means(g + 1, round_after(n, q), (q + 1) % RING)
                mixing(3)
                if not beyond(g, NG - 1):
                    group_squares(g + 1, (q + 1) % RING)

            act.wait_ge(s_con, 1)
            group_means(0, 0, 0)
            group_squares(0, 0)
            sweep(act, NG - 1, step)
            step(NG - 1, (NG - 1) // RING, (NG - 1) % RING)
            for j in range(G):
                scale_bases(NG - 1, (NG - 1) % RING, j)

            def window_std(g, q):
                r = q % NRING
                act.wait_ge(n_mv, g + 1)
                nc.scalar.activation(nstd[:, r, :], nmv[:, r, :, 1], ACT.Sqrt, bias=eps_col[:, 0:1]).then_inc(n_std, 1)

            def node_step(g, n, q, ahead=True):
                r = q % NRING
                act.wait_ge(n_shift, g + 1)
                if not is_before(g, NRING):
                    act.wait_ge(n_hT, g - (NRING - 1))
                for j in range(G):
                    ins = nc.scalar.activation(hw[:, r, j, :], xw[:, q, j, :], ACT.Relu, bias=shift[:, r, j:j + 1],
                                               scale=nrstd[:, r, j:j + 1])
                ins.then_inc(n_h, 1)
                if ahead:
                    window_std(g + 1, q + 1)
                act.wait_ge(n_hT, g + 1)
                if not is_before(g, NRING):
                    act.wait_ge(n_y, g - (NRING - 1))
                nc.scalar.activation(hwT[:, r, :, :], hwT_ps[q % 2], ACT.Copy).then_inc(n_hT_sb, 1)

            window_std(0, 0)
            sweep(act, NGW - 1, node_step, LRING, LRING)
            node_step(NGW - 1, (NGW - 1) // LRING, (NGW - 1) % LRING, False)

        @block.tensor
        def _(pe):
            pe.wait_ge(s_meta, 1)

            def count(t, first, last):
                return nc.tensor.matmul(mix_ps[0:HI, 256:256 + LO], hi_hot[:, :, t], lo_hot[:, :, t],
                                        start=first, stop=last)

            for t in range(NT):
                mm = count(t, t == 0, t == NT - 1)
            mm.then_inc(s_hist, 1)
            pe.wait_ge(s_wt, 16 * (3 + G))

            def products(g, q, j):
                r = (q * G + j) % RING
                if not is_before(g, 1) or j >= RING:
                    pe.wait_ge(s_a, g * (2 * G) + 2 * (j - RING + 1))
                for b0, done in ((B // 2, s_y_high), (0, s_y)):
                    nc.tensor.matmul(y_ps[r][:, b0:b0 + B // 2, :], hT[:, q, j, :],
                                     w_all[:, b0:b0 + B // 2, :], start=True, stop=True).then_inc(done, 1)

            def step(g, n, q):
                def messages(j):
                    if not is_before(g, 1):
                        if j == 0:
                            pe.wait_ge(s_hT_sb, g)
                        products(g - 1, (q - 1) % RING, j)

                messages(0)
                messages(1)
                pe.wait_ge(s_hot, g + 1)
                if not is_before(g, 1):
                    pe.wait_ge(s_mix, g)
                nc.tensor.transpose(mix_ps[:, 0:P], hot[:, q, :, :].rearrange("p t r -> p (t r)"),
                                    ident[:, :]).then_inc(s_hotT, 1)
                messages(2)
                pe.wait_ge(s_hotT_sb, g + 1)
                nc.tensor.matmul(mix_ps[:, P:P + G * B], hotT[:, q, :], w_mix[:, :],
                                 start=True, stop=True).then_inc(s_mix_ps, 1)
                pe.wait_ge(s_relu, g * G + G)
                for j in range(G):
                    mm = nc.tensor.transpose(hT_ps[:, j, :], h[:, q, j, :], ident[:, :])
                mm.then_inc(s_hT, 1)
                messages(3)

            sweep(pe, NG - 1, step)
            pe.wait_ge(s_meta, 2)
            nc.tensor.matmul(mix_ps[0:HI, 300:301], above[0:HI, 0:HI], upto[:, LO - 1:LO], start=True, stop=True)
            nc.tensor.matmul(mix_ps[:, 302:303], ones[:, :], bad[:, 3:4], start=True, stop=True).then_inc(s_off, 1)
            pe.wait_ge(s_meta, 3)
            step(NG - 1, (NG - 1) // RING, (NG - 1) % RING)
            pe.wait_ge(s_hT_sb, NG)
            for j in range(G):
                products(NG - 1, (NG - 1) % RING, j)

            pe.wait_ge(s_tab, 48)
            with pe.If(pe.value_load(mode, min_val=0, max_val=1) > 0):
                with pe.Fori(0, NT) as t:
                    pe.wait_ge(c_dst, t + 1)
                    nc.tensor.transpose(hT_ps[:, 0, :], cdst[:, :], ident[:, :]).then_inc(c_row, 1)
                    pe.wait_ge(c_v, t * 7 + 1)
                    nc.tensor.matmul(mix_ps[:, 0:F], ceq[:, :], cm[:, 0:F], start=True, stop=True).then_inc(c_sum, 1)

            def window_sums(g, q, windows=G):
                r = q % NRING
                pe.wait_ge(n_hT_sb, g + 1)
                pe.wait_ge(n_pick, g + 1)
                if not is_before(g, NRING):
                    pe.wait_ge(n_res, g - (NRING - 1))
                for j in range(windows):
                    y = win_ps[r][:, j, :]
                    nc.tensor.matmul(y, hwT[:, r, j, :], w_loop[:, :], start=True, stop=False)
                    nc.tensor.matmul(y, pick[:, r, j, 0, :][0:SEG_P], seg[0:SEG_P, q, j, 0, 0:F],
                                     start=False, stop=False)
                    mm = nc.tensor.matmul(y, pick[:, r, j, 1, :][0:SEG_P + 1], seg[0:SEG_P + 1, q, j, 1, 0:F],
                                          start=False, stop=True)
                mm.then_inc(n_y, 1)

            def node_step(g, n, q):
                pe.wait_ge(n_h, g + 1)
                if not is_before(g, 2):
                    pe.wait_ge(n_hT_sb, g - 1)
                for j in range(G):
                    mm = nc.tensor.transpose(hwT_ps[q % 2][:, j, :], hw[:, q % NRING, j, :], ident[:, :])
                mm.then_inc(n_hT, 1)
                if not is_before(g, 1):
                    window_sums(g - 1, (q - 1) % LRING)

            sweep(pe, NGW, node_step, LRING, LRING)
            g = NGW - 1
            window_sums(g, g % LRING, LAST_FULL + 1)

        @block.vector
        def _(dve):
            nc.vector.memset(ones[:, :], 1.0)
            nc.vector.memset(eps_col[:, :], EPS)
            nc.vector.memset(bad[:, :], 0.0)
            nc.vector.memset(pick[SEG_P:P, :, :, :, :], 1.0)
            dve.wait_ge(s_cst, 3)
            nc.vector.tensor_copy(iota_n[:, :], iota_i[:, :])
            nc.vector.tensor_copy(part_f[:, :], part_i[:, :])
            nc.vector.tensor_copy(win_off[:, :], win_i[:, :]).then_inc(s_num, 1)
            dve.wait_ge(s_num, 1)
            nc.vector.tensor_scalar(ident[:, :], iota_n[:, :], part_f[:, 0:1], None, ALU.is_equal)
            nc.vector.tensor_scalar(above[:, :], iota_n[:, :], part_f[:, 0:1], None, ALU.is_gt)
            nc.vector.tensor_scalar(below[:, :], iota_n[:, :], part_f[:, 0:1], None, ALU.is_lt)
            dve.wait_ge(s_ld, 16 * 8)
            nc.vector.tensor_copy(type_f[:, :], type_i[:, :])
            nc.vector.tensor_copy(next_f[:, :], next_i[:, :])
            nc.vector.tensor_copy(dst_f[:, :], dst_i[:, :]).then_inc(s_con, 1)

            def after(ins):
                done[0] += 1
                ins.then_inc(s_num, 1)

            def settle():
                dve.wait_ge(s_num, done[0])

            done = [1]
            nc.vector.tensor_scalar(lo_i[:, :], dst_i[:, :], P.bit_length() - 1, LO - 1,
                                    ALU.logical_shift_right, ALU.bitwise_and)
            after(nc.vector.tensor_scalar(hi_i[:, :], dst_i[:, :], (P * LO).bit_length() - 1, None,
                                          ALU.logical_shift_right))
            settle()
            nc.vector.tensor_copy(lo_b[:, :], lo_i[:, :])
            after(nc.vector.tensor_copy(hi_b[:, :], hi_i[:, :]))
            settle()
            for v in range(LO):
                nc.vector.tensor_scalar(lo_hot[:, v, :], lo_b[:, :], float(v), None, ALU.is_equal)
            for v in range(HI):
                ins = nc.vector.tensor_scalar(hi_hot[:, v, :], hi_b[:, :], float(v), None, ALU.is_equal)
            ins.then_inc(s_meta, 1)
            dve.wait_ge(s_con, 1)
            nc.vector.tensor_tensor(falls[:, 0:NT - 1], dst_f[:, 0:NT - 1], dst_f[:, 1:NT], ALU.is_gt)
            after(nc.vector.tensor_tensor(falls[:, NT - 1:NT], dst_f[:, NT - 1:NT], next_f[:, :], ALU.is_gt))
            settle()
            after(nc.vector.tensor_reduce(bad[:, 0:1], falls[:, :], AX_X, ALU.max))
            def add(acc, r, c, base, first):
                return nc.vector.scalar_tensor_tensor(out=acc, in0=y_ps[r][:, base, :], scalar=c[:, base:base + 1],
                                                      in1=first, op0=ALU.mult, op1=ALU.add)

            def sum_high(g, q, j, base):
                r, before = (q * G + j) % RING, g * (3 * G) + 3 * j + (base - 5)
                if base == 5:
                    dve.wait_ge(s_z_high, g * G + j + 1)
                    first = z[:, r, 2, :]
                    if not is_before(g, 1) or j >= RING:
                        dve.wait_ge(s_msg, g * G + j - (RING - 1))
                else:
                    dve.wait_ge(s_b, before)
                    first = sum_b[:, r, :]
                add(sum_b[:, r, :], r, mix[:, q, j, :], base, first).then_inc(s_b, 1)

            def sum_low(g, q, j, base):
                r, before = (q * G + j) % RING, g * (2 * G) + 2 * j + (base - 2)
                if base == 2:
                    dve.wait_ge(s_u, g * G + j + 1)
                    first = u[:, r, :]
                else:
                    dve.wait_ge(s_b, g * (3 * G) + 3 * j + 3)
                    dve.wait_ge(s_a, before)
                    first = sum_a[:, r, :]
                add(sum_a[:, r, :], r, mix[:, q, j, :], base, first).then_inc(s_a, 1)

            def message(g, n, q, j):
                r = (q * G + j) % RING
                if j == 0 and not is_before(g, RING):
                    dve.wait_ge(s_mst[q], n * 16)
                dve.wait_ge(s_a, g * (2 * G) + 2 * j + 2)
                nc.vector.tensor_tensor(msg[:, q, j, 0:F], sum_a[:, r, :], sum_b[:, r, :], ALU.add).then_inc(s_msg, 1)

            def tile_slot(g, n, q, j, more):
                now = not is_before(g, 1) and not beyond(g, NG + 1)
                p = g - 1, round_before(n, q), (q - 1) % RING
                b = p if j else (g - 2, round_before(n, q, 2), (q - 2) % RING)
                bj = (j - 1) % G
                past = not is_before(g, 1 if j else 2)
                an, aq = round_after(n, q), (q + 1) % RING
                if now:
                    sum_high(p[0], p[2], j, 5)
                if past:
                    sum_low(b[0], b[2], bj, 2)
                if now:
                    sum_high(p[0], p[2], j, 6)
                if past:
                    sum_low(b[0], b[2], bj, 3)
                if more:
                    dve.wait_ge(s_gather[aq * G + j], an * 16 + 16)
                    if j == 0 and not is_before(g, RING - 1):
                        dve.wait_ge(s_bn, g * (2 * DV) - (RING - 2) * (2 * DV))
                        dve.wait_ge(s_std, g - (RING - 2))
                        dve.wait_ge(s_relu, g * G - (RING - 2) * G)
                    nc.vector.bn_stats(stats[:, aq, j, :], xg[:, aq, j, :]).then_inc(s_bn, 1)
                if now:
                    sum_high(p[0], p[2], j, 7)
                if more:
                    dve.wait_ge(s_bn, g * (2 * DV) + (2 * DV + 2 * j + 1))
                if past:
                    message(*b, bj)
                elif more:
                    hold(dve, passed["dve"])
                if more:
                    nc.vector.bn_aggr(mv[:, aq, j, :], stats[:, aq, j, :]).then_inc(s_bn, 1)

            def one_hot(g, q):
                if not is_before(g, RING):
                    dve.wait_ge(s_hotT, g - (RING - 1))
                nc.vector.tensor_tensor(hot[:, q, :, :],
                                        type_f[:, bass.ds(g * G, G)].unsqueeze(2).to_broadcast([P, G, R]),
                                        iota_n[:, 0:R].unsqueeze(1).to_broadcast([P, G, R]),
                                        ALU.is_equal).then_inc(s_hot, 1)

            def means(g, q):
                dve.wait_ge(s_bn, g * (2 * DV) + 2 * DV)
                nc.vector.tensor_scalar(neg_mean[:, q, 0:DV], mv[:, q, :, 0], -1.0, None, ALU.mult).then_inc(s_mean, 1)

            def step(g, n, q):
                more, here = not beyond(g, NG - 1), not beyond(g, NG)
                tile_slot(g, n, q, 0, more)
                tile_slot(g, n, q, 1, more)
                if here:
                    dve.wait_ge(s_std, g + 1)
                    if not is_before(g, RING):
                        dve.wait_ge(s_gain, g - (RING - 1))
                    nc.vector.reciprocal(rstd[:, q, :], std[:, q, :]).then_inc(s_rstd, 1)
                if more:
                    means(g + 1, (q + 1) % RING)
                tile_slot(g, n, q, 2, False)
                if here:
                    dve.wait_ge(s_gain, g + 1)
                    dve.wait_ge(s_mix_ps, g + 1)
                    nc.vector.tensor_tensor(mix[:, q, :, :],
                                            mix_ps[:, P:P + G * B].rearrange("p (t b) -> p t b", t=G),
                                            gain[:, q, :].unsqueeze(2).to_broadcast([P, G, B]),
                                            ALU.mult).then_inc(s_mix, 1)
                tile_slot(g, n, q, 3, False)
                if more:
                    one_hot(g + 1, (q + 1) % RING)

            for j in range(DV):
                dve.wait_ge(s_gather[j], 16)
                nc.vector.bn_stats(stats[:, 0, j, :], xg[:, 0, j, :]).then_inc(s_bn, 1)
                dve.wait_ge(s_bn, 2 * j + 1)
                nc.vector.bn_aggr(mv[:, 0, j, :], stats[:, 0, j, :]).then_inc(s_bn, 1)
            one_hot(0, 0)
            means(0, 0)
            sweep(dve, NG - 1, step)

            dve.wait_ge(s_hist, 1)
            after(nc.vector.tensor_copy(hist[:, :], mix_ps[0:HI, 256:256 + LO]))
            settle()
            nc.vector.tensor_tensor_scan(upto[:, :], ones[0:HI, 0:LO], hist[:, :], 0.0, ALU.mult, ALU.add)
            after(nc.vector.tensor_scalar(big[:, :], hist[:, :], float(SEG), None, ALU.is_gt))
            settle()
            after(nc.vector.tensor_reduce(bad[0:HI, 1:2], big[:, :], AX_X, ALU.max))
            settle()
            nc.vector.tensor_tensor(bad[:, 3:4], bad[:, 0:1], bad[:, 1:2], ALU.add).then_inc(s_meta, 1)
            dve.wait_ge(s_off, 1)
            after(nc.vector.tensor_copy(before[:, :], mix_ps[0:HI, 300:301]))
            nc.vector.tensor_scalar(mode_f[:, :], mix_ps[:, 302:303], 0.5, None, ALU.is_gt).then_inc(s_meta, 1)
            nc.vector.tensor_scalar(big[:, :], part_f[0:HI, 0:1].to_broadcast([HI, LO]), float(LO * P), float(EP),
                                    ALU.mult, ALU.add)
            settle()
            after(nc.vector.scalar_tensor_tensor(out=start[:, :], in0=upto[:, :], scalar=before[:, 0:1],
                                                 in1=hist[:, :], op0=ALU.add, op1=ALU.subtract))
            settle()
            nc.vector.tensor_scalar(start_c[:, :], start[:, :], float(EP - SEG), None, ALU.min)
            after(nc.vector.scalar_tensor_tensor(out=hist[:, :], in0=iota_n[0:HI, 0:LO], scalar=float(P),
                                                 in1=big[:, :], op0=ALU.mult, op1=ALU.add))
            settle()
            after(nc.vector.tensor_tensor(upto[:, :], hist[:, :], start_c[:, :], ALU.subtract))
            settle()
            nc.vector.tensor_copy(mode_i[:, :], mode_f[:, :])
            nc.vector.scalar_tensor_tensor(out=start_i[:, :], in0=upto[:, :], scalar=mode_f[0:HI, 0:1],
                                           in1=start_c[:, :], op0=ALU.mult, op1=ALU.add).then_inc(s_start, 1)

            step(NG - 1, (NG - 1) // RING, (NG - 1) % RING)
            step(NG, NG // RING, NG % RING)
            last = NG - 1, (NG - 1) // RING, (NG - 1) % RING
            sum_low(last[0], last[2], G - 1, 2)
            sum_low(last[0], last[2], G - 1, 3)
            message(*last, G - 1)

            dve.wait_ge(s_tab, 48)
            with dve.If(dve.value_load(mode, min_val=0, max_val=1) > 0):
                nc.vector.memset(cz[:, 0:F], 0.0)
                nc.vector.tensor_scalar(cz[:, F:C], part_f[:, :], -float(P), None, ALU.add).then_inc(c_own, 1)
                with dve.Fori(0, NW + 2) as w:
                    dve.wait_ge(c_own, w + 1)
                    nc.vector.tensor_scalar(cz[:, F:C], cz[:, F:C], float(P), None, ALU.add).then_inc(c_own, 1)
                    dve.wait_ge(c_own, w + 2)
                    nc.vector.tensor_copy(cc[:, 7:8], cz[:, F:C]).then_inc(c_zero, 1)
                    dve.wait_ge(c_zst, w * 16 + 16)
                    hold(dve, passed["dve"])
                with dve.Fori(0, NT) as t:
                    tile_dst = cm[:, F:C]
                    dve.wait_ge(c_ld, t * 16 + 16)
                    nc.vector.tensor_scalar(cdst[:, :], ones[:, :], tile_dst, None, ALU.mult).then_inc(c_dst, 1)
                    dve.wait_ge(c_row, t + 1)
                    nc.vector.tensor_scalar(ceq[:, :], hT_ps[:, 0, :], tile_dst, None, ALU.is_equal).then_inc(c_v, 1)
                    nc.vector.tensor_scalar(cc[:, 1:2], tile_dst, N - 0.5, None, ALU.is_gt).then_inc(c_v, 1)
                    nc.vector.scalar_tensor_tensor(out=cc[:, 3:4], in0=part_f[:, :], scalar=float(DUMMY - EP),
                                                   in1=tile_dst, op0=ALU.add, op1=ALU.subtract).then_inc(c_v, 1)
                    dve.wait_ge(c_v, t * 7 + 3)
                    nc.vector.tensor_tensor(cwork[:, :], ceq[:, :], below[:, :], ALU.mult).then_inc(c_v, 1)
                    dve.wait_ge(c_v, t * 7 + 4)
                    nc.vector.tensor_reduce(cc[:, 0:1], cwork[:, :], AX_X, ALU.add).then_inc(c_v, 1)
                    dve.wait_ge(c_v, t * 7 + 5)
                    nc.vector.scalar_tensor_tensor(out=cc[:, 2:3], in0=cc[:, 0:1], scalar=1.0, in1=cc[:, 1:2],
                                                   op0=ALU.min, op1=ALU.max).then_inc(c_v, 1)
                    dve.wait_ge(c_v, t * 7 + 6)
                    nc.vector.tensor_tensor(cc[:, 4:5], cc[:, 2:3], cc[:, 3:4], ALU.mult).then_inc(c_v, 1)
                    dve.wait_ge(c_v, t * 7 + 7)
                    nc.vector.scalar_tensor_tensor(out=cidx[:, :], in0=tile_dst, scalar=float(EP), in1=cc[:, 4:5],
                                                   op0=ALU.add, op1=ALU.add).then_inc(c_idx, 1)
                    dve.wait_ge(c_cur, t * 16 + 16)
                    dve.wait_ge(c_sum, t + 1)
                    nc.vector.tensor_tensor(ccur[:, 0:F], ccur[:, 0:F], mix_ps[:, 0:F], ALU.add).then_inc(c_new, 1)

            def window_stats(g, n, q, windows, x_loads):
                r = q % NRING
                dve.wait_ge(n_x[q], n * 16 + 16 * x_loads)
                for j in range(G):
                    ins = nc.vector.bn_stats(nstats[:, r, j, :], xw[:, q, j, :])
                ins.then_inc(n_bn, 1)
                dve.wait_ge(n_seg[q], n * (16 * G) + 16 * windows)
                if not is_before(g, NRING):
                    dve.wait_ge(n_y, g - (NRING - 1))
                nc.vector.tensor_tensor(rel[:, r, 0:windows, :], seg[0:SEG_P, q, 0:windows, :, F],
                                        win_off[0:SEG_P, bass.ds(g * G, windows)].unsqueeze(2).to_broadcast(
                                            [SEG_P, windows, CHUNKS]), ALU.subtract).then_inc(n_rel, 1)
                dve.wait_ge(n_bn, g + 1)
                hold(dve, passed["dve"])
                for j in range(G):
                    ins = nc.vector.bn_aggr(nmv[:, r, j, :], nstats[:, r, j, :])
                ins.then_inc(n_mv, 1)
                shape = [SEG_P, windows * CHUNKS, P]
                dve.wait_ge(n_rel, g + 1)
                nc.vector.tensor_tensor(
                    pick[0:SEG_P, r, 0:windows, :, :].rearrange("p j c n -> p (j c) n"),
                    iota_n[0:SEG_P, :].unsqueeze(1).to_broadcast(shape),
                    rel[:, r, 0:windows, :].rearrange("p j c -> p (j c)").unsqueeze(2).to_broadcast(shape),
                    ALU.is_equal).then_inc(n_pick, 1)
                dve.wait_ge(n_std, g + 1)
                nc.vector.reciprocal(nrstd[:, r, :], nstd[:, r, :]).then_inc(n_rstd, 1)

            def window_shift(g, q):
                r = q % NRING
                dve.wait_ge(n_rstd, g + 1)
                nc.vector.scalar_tensor_tensor(out=shift[:, r, :], in0=nmv[:, r, :, 0], scalar=-1.0,
                                               in1=nrstd[:, r, :], op0=ALU.mult, op1=ALU.mult).then_inc(n_shift, 1)

            def results(g, n, q, windows=G):
                r = q % NRING
                dve.wait_ge(n_y, g + 1)
                if not is_before(g, NRING):
                    dve.wait_ge(n_out[r], n * (16 * LRING // NRING) + 16 * (q // NRING))
                nc.vector.scalar_tensor_tensor(out=res[:, r, 0:windows, :], in0=win_ps[r][:, 0:windows, :], scalar=0.0,
                                               in1=xw[:, q, 0:windows, :], op0=ALU.max,
                                               op1=ALU.add).then_inc(n_res, 1)

            def node_step(g, n, q, windows=G, x_loads=1):
                ahead_q = (q + 1) % LRING
                window_stats(g + 1, round_after(n, q, LRING), ahead_q, windows, x_loads)
                if not is_before(g, 2):
                    results(g - 2, round_before(n, q, 2, LRING), (q - 2) % LRING)
                window_shift(g + 1, ahead_q)

            window_stats(0, 0, 0, G, 1)
            window_shift(0, 0)
            sweep(dve, NGW - 2, node_step, LRING, LRING)
            g = NGW - 2
            node_step(g, g // LRING, g % LRING, LAST_FULL + 1, 1 + (LAST_FULL > 0))
            for g in (NGW - 3, NGW - 2):
                results(g, g // LRING, g % LRING)
            g = NGW - 1
            results(g, g // LRING, g % LRING, LAST_FULL + 1)


_INS = ["x", "src", "dst", "edge_type_32", "edge_weight1", "L0_gnn_weight", "L0_gnn_w_comp", "L0_gnn_loop_weight",
        "L0_gnn_h_bias"]


def kernel(**inputs):
    import concourse.bacc as bacc
    from concourse.bass_utils import run_bass_kernel_spmd

    nc = bacc.Bacc("TRN2", target_bir_lowering=False, num_devices=1)
    arrays, args = {}, []
    for name in _INS:
        a = np.ascontiguousarray(inputs[name])
        arrays[name] = a
        args.append(nc.dram_tensor(name, a.shape, mybir.dt.from_np(a.dtype), kind="ExternalInput").ap())
    args.append(nc.dram_tensor("out", inputs["x"].shape, F32, kind="ExternalOutput").ap())
    build_layer(nc, *args)
    r = run_bass_kernel_spmd(nc, [arrays], core_ids=[0])
    return r.results[0]["out"]
```

```python
from contextlib import ExitStack

import numpy as np

import concourse.bass as bass
from concourse import mybir

ALU = mybir.AluOpType
ACT = mybir.ActivationFunctionType
F32 = mybir.dt.float32
BF16 = mybir.dt.bfloat16
I32 = mybir.dt.int32
AX_X = mybir.AxisListType.X

P = 128
G = 4
RING = 3
EPS = 1e-5
CHUNKS = 2
DV = 2
NRING = 4
LRING = 8
SEG_P = 96


def sweep(eng, count, step, ring=RING, peel=5, first=0):
    for g in range(first, min(peel, count)):
        step(g, g // ring, g % ring)
    rounds = max(0, (count - peel) // ring)
    if rounds:
        with eng.Fori(0, rounds) as i:
            for k in range(peel, peel + ring):
                step(i * ring + k, i + k // ring, k % ring)
    for g in range(peel + ring * rounds, count):
        step(g, g // ring, g % ring)


def hold(eng, passed):
    eng.sem_inc(passed, 1)


def round_before(n, q, k=1, ring=RING):
    return n + (q - k) // ring


def round_after(n, q, ring=RING):
    return n + (q + 1) // ring


def beyond(g, n):
    return isinstance(g, int) and g >= n


def is_before(g, n):
    return isinstance(g, int) and g < n


def build_layer(nc, x, src, dst, etype, norm, weight, w_comp, loop_weight, bias, out):
    N, D = x.shape
    E = src.shape[0]
    R, B = w_comp.shape
    F = loop_weight.shape[1]
    NT = -(-E // P)
    NT = -(-NT // G) * G
    NG = NT // G
    EP = NT * P
    FULL_P, REST = E // NT, E % NT
    NW = -(-N // P)
    LAST = N - (NW - 1) * P
    NGW = -(-NW // G)
    SEG = SEG_P * CHUNKS
    LO = 32
    HI = -(-(NW + 1) // LO)
    DST_PAD = HI * LO * P - 1
    NODE_ROWS = (NW + 1) * P
    DUMMY = EP + NODE_ROWS
    ROWS = DUMMY + P
    C = F + 1
    assert D == P and F == P and R * G == P and 2 * G * P <= 1024 and B == 8
    assert REST > 0 and EP - E <= SEG and NG > RING and NGW > LRING and LRING % NRING == 0

    msgs = nc.dram_tensor("msgs", [ROWS, C], F32, kind="Internal").ap()
    first_row = nc.dram_tensor("first_row", [HI * LO, 1], I32, kind="Internal").ap()
    mode = nc.dram_tensor("mode", [1, 1], I32, kind="Internal").ap()

    ctx = ExitStack()
    with ctx:
        def sb(name, shape, dt=F32):
            return ctx.enter_context(nc.sbuf_tensor(name, shape, dt))

        def psum(name, shape, dt=F32):
            return ctx.enter_context(nc.psum_tensor(name, shape, dt))

        def sem(name):
            return ctx.enter_context(nc.semaphore(name))

        iota_i = sb("iota_i", [P, P], I32)
        part_i = sb("part_i", [P, 1], I32)
        iota_n = sb("iota_n", [P, P])
        part_f = sb("part_f", [P, 1])
        ident = sb("ident", [P, P])
        above = sb("above", [P, P])
        below = sb("below", [P, P])
        ones = sb("ones", [P, P])
        eps_col = sb("eps_col", [P, 1])
        win_i = sb("win_i", [P, NGW * G], I32)
        win_off = sb("win_off", [P, NGW * G])
        w_all = sb("w_all", [P, B, F])
        w_loop = sb("w_loop", [P, F])
        w_mix = sb("w_mix", [P, G * B])
        src_all = sb("src_all", [P, NT], I32)
        type_i = sb("type_i", [P, NT], I32)
        type_f = sb("type_f", [P, NT])
        norm_all = sb("norm_all", [P, NT])
        dst_i = sb("dst_i", [P, NT], I32)
        dst_f = sb("dst_f", [P, NT])
        next_i = sb("next_i", [P, 1], I32)
        next_f = sb("next_f", [P, 1])
        hi_i = sb("hi_i", [P, NT], I32)
        lo_i = sb("lo_i", [P, NT], I32)
        hi_b = sb("hi_b", [P, NT], BF16)
        lo_b = sb("lo_b", [P, NT], BF16)
        hi_hot = sb("hi_hot", [P, HI, NT], BF16)
        lo_hot = sb("lo_hot", [P, LO, NT], BF16)
        falls = sb("falls", [P, NT])
        bad = sb("bad", [P, 4])
        hist = sb("hist", [HI, LO])
        upto = sb("upto", [HI, LO])
        start = sb("start", [HI, LO])
        start_c = sb("start_c", [HI, LO])
        start_i = sb("start_i", [HI, LO], I32)
        before = sb("before", [HI, 1])
        big = sb("big", [HI, LO])
        row_tab = sb("row_tab", [1, HI * LO], I32)
        mode_f = sb("mode_f", [P, 1])
        mode_i = sb("mode_i", [P, 1], I32)
        xg = sb("xg", [P, RING, G, D])
        stats = sb("stats", [P, RING, DV, 6])
        mv = sb("mv", [P, RING, DV, 2])
        squares = sb("squares", [P, RING, G - DV])
        neg_mean = sb("neg_mean", [P, RING, G])
        std = sb("std", [P, RING, G])
        h = sb("h", [P, RING, G, D])
        hT = sb("hT", [P, RING, G, P])
        idx = sb("idx", [P, RING, G], I32)
        hot = sb("hot", [P, RING, G, R])
        hotT = sb("hotT", [P, RING, P])
        rstd = sb("rstd", [P, RING, G])
        gain = sb("gain", [P, RING, G])
        mix = sb("mix", [P, RING, G, B])
        z = sb("z", [P, RING, 3, F])
        u = sb("u", [P, RING, F])
        sum_a = sb("sum_a", [P, RING, F])
        sum_b = sb("sum_b", [P, RING, F])
        msg = sb("msg", [P, RING, G, C])
        xw = sb("xw", [P, LRING, G, D])
        nstats = sb("nstats", [P, NRING, G, 6])
        nmv = sb("nmv", [P, NRING, G, 2])
        nstd = sb("nstd", [P, NRING, G])
        nrstd = sb("nrstd", [P, NRING, G])
        shift = sb("shift", [P, NRING, G])
        hw = sb("hw", [P, NRING, G, D])
        hwT = sb("hwT", [P, NRING, G, P])
        seg = sb("seg", [P, LRING, G, CHUNKS, C])
        rel = sb("rel", [SEG_P, NRING, G, CHUNKS])
        pick = sb("pick", [P, NRING, G, CHUNKS, P])
        res = sb("res", [P, NRING, G, F])
        cz = sb("cz", [P, C])
        cm = sb("cm", [P, C])
        ccur = sb("ccur", [P, C])
        cdst = sb("cdst", [P, P])
        ceq = sb("ceq", [P, P])
        cwork = sb("cwork", [P, P])
        cc = sb("cc", [P, 8])
        cidx = sb("cidx", [P, 1], I32)

        y_ps = [psum(f"y_ps{r}", [P, B, F]) for r in range(RING)]
        hT_ps = psum("hT_ps", [P, G, P])
        mix_ps = psum("mix_ps", [P, 512])

        win_ps = [y_ps[0][:, 0:G, :], y_ps[1][:, 0:G, :], y_ps[2][:, 0:G, :], y_ps[0][:, G:2 * G, :]]
        hwT_ps = [hT_ps[:, :, :], mix_ps[:, :].rearrange("p (t e) -> p t e", t=G)]

        s_iotas = sem("s_iotas")
        passed = {e: sem(f"passed_{e}") for e in ("sp", "pool", "dve")}
        s_padded = sem("s_padded")
        s_step = sem("s_step")
        s_src = sem("s_src")
        s_edges = sem("s_edges")
        s_weights = sem("s_weights")
        s_floats = sem("s_floats")
        s_meta = sem("s_meta")
        s_hist = sem("s_hist")
        s_start = sem("s_start")
        s_off = sem("s_off")
        s_table = sem("s_table")
        s_idx = sem("s_idx")
        s_gather = [sem(f"s_gather{i}") for i in range(RING * G)]
        s_bn = sem("s_bn")
        s_mean = sem("s_mean")
        s_mean_act = sem("s_mean_act")
        s_squares = sem("s_squares")
        s_hot = sem("s_hot")
        s_std = sem("s_std")
        s_rstd = sem("s_rstd")
        s_gain = sem("s_gain")
        s_mix = sem("s_mix")
        s_relu = sem("s_relu")
        s_hotT = sem("s_hotT")
        s_hotT_sb = sem("s_hotT_sb")
        s_mix_ps = sem("s_mix_ps")
        s_hT = sem("s_hT")
        s_hT_sb = sem("s_hT_sb")
        s_y_high = sem("s_y_high")
        s_y = sem("s_y")
        s_z_high = sem("s_z_high")
        s_z = sem("s_z")
        s_u = sem("s_u")
        s_a = sem("s_a")
        s_b = sem("s_b")
        s_msg = sem("s_msg")
        s_dst_col = sem("s_dst_col")
        s_stored = [sem(f"s_stored{q}") for q in range(RING)]
        c_zero = sem("c_zero")
        c_zero_st = sem("c_zero_st")
        c_load = sem("c_load")
        c_dst = sem("c_dst")
        c_row = sem("c_row")
        c_step = sem("c_step")
        c_sum = sem("c_sum")
        c_idx = sem("c_idx")
        c_cur = sem("c_cur")
        c_new = sem("c_new")
        c_own = sem("c_own")
        c_st = sem("c_st")
        n_x = [sem(f"n_x{q}") for q in range(LRING)]
        n_seg = [sem(f"n_seg{q}") for q in range(LRING)]
        n_bn = sem("n_bn")
        n_mv = sem("n_mv")
        n_std = sem("n_std")
        n_rstd = sem("n_rstd")
        n_shift = sem("n_shift")
        n_h = sem("n_h")
        n_pick = sem("n_pick")
        n_rel = sem("n_rel")
        n_hT = sem("n_hT")
        n_hT_sb = sem("n_hT_sb")
        n_y = sem("n_y")
        n_res = sem("n_res")
        n_out = [sem(f"n_out{q}") for q in range(NRING)]

        def edges(a):
            return (a[0:FULL_P * NT].rearrange("(p t) -> p t", t=NT),
                    a[FULL_P * NT:E].rearrange("(p t) -> p t", p=1))

        def load_edges(eng, tile, a, s):
            full, rest = edges(a)
            eng.dma_start(tile[0:FULL_P, :], full).then_inc(s, 16)
            eng.dma_start(tile[FULL_P:FULL_P + 1, 0:REST], rest).then_inc(s, 16)

        msg_rows = msgs[0:EP, :].rearrange("(p t) c -> p (t c)", t=NT)
        start_flat = first_row.rearrange("(a b) c -> a (b c)", b=LO)
        X_WIN = x[0:(NW - 1) * P, :].rearrange("(w p) d -> p w d", p=P)
        OUT_WIN = out[0:(NW - 1) * P, :].rearrange("(w p) d -> p w d", p=P)
        LAST_FULL = NW - 1 - (NGW - 1) * G

        block = ctx.enter_context(nc.Block())

        @block.sync
        def _(sp):
            sp.wait_ge(s_padded, 1)
            load_edges(sp, src_all, src, s_src)
            sp.wait_ge(s_padded, 6)
            load_edges(sp, dst_i, dst, s_edges)
            sp.dma_start(next_i[0:FULL_P - 1, :],
                         dst[NT:FULL_P * NT].rearrange("(p t) -> p t", t=NT)[:, 0:1],
                         allow_slow_non_contiguous=True).then_inc(s_edges, 16)
            sp.dma_start(next_i[FULL_P - 1:FULL_P, :],
                         dst[FULL_P * NT:FULL_P * NT + 1].rearrange("(p t) -> p t", p=1)).then_inc(s_edges, 16)
            load_edges(sp, type_i, etype, s_edges)
            load_edges(sp, norm_all, norm.rearrange("e o -> (e o)"), s_edges)
            sp.dma_start(w_all[:, :, :], weight.rearrange("b d f -> d b f")).then_inc(s_weights, 16)
            sp.dma_start(w_loop[:, :], loop_weight).then_inc(s_weights, 16)
            for j in range(G):
                sp.dma_start(w_mix[R * j:R * j + R, B * j:B * j + B], w_comp).then_inc(s_weights, 16)
            sp.dma_start(seg[SEG_P:SEG_P + 1, :, :, CHUNKS - 1, 0:F].rearrange("p q j f -> p (q j) f"),
                         bias.rearrange("(a b f) -> a b f", a=1, b=1).to_broadcast([1, LRING * G, F])
                         ).then_inc(s_weights, 16)

            def store_messages(g, n, q):
                sp.wait_ge(s_msg, g * G + G)
                hold(sp, passed["sp"])
                sp.wait_ge(s_dst_col, g + 1)
                hold(sp, passed["sp"])
                sp.dma_start(msg_rows[:, bass.ds(g * (G * C), G * C)],
                             msg[:, q, :, :].rearrange("p t c -> p (t c)")).then_inc(s_stored[q], 16)

            sweep(sp, NG - 3, store_messages)
            sp.wait_ge(s_start, 1)
            sp.dma_start(start_flat, start_i[:, :]).then_inc(s_table, 16)
            sp.dma_start(mode, mode_i[0:1, :]).then_inc(s_table, 16)
            sp.wait_ge(s_table, 32)
            sp.dma_start(row_tab[:, :], first_row.rearrange("w c -> c w")).then_inc(s_table, 16)
            for g in range(NG - 3, NG):
                store_messages(g, g // RING, g % RING)
            for q in range(RING):
                sp.wait_ge(s_stored[q], 16 * len(range(q, NG, RING)))

            sp.wait_ge(s_table, 48)
            with sp.If(sp.value_load(mode, min_val=0, max_val=1) > 0):
                with sp.Fori(0, NW + 2) as w:
                    sp.wait_ge(c_zero, w + 1)
                    hold(sp, passed["sp"])
                    sp.dma_start(msgs[bass.ds(w * P + EP, P), :], cz[:, :]).then_inc(c_zero_st, 16)
                with sp.Fori(0, NT) as t:
                    sp.dma_start(cm[:, :], msgs[bass.ds(t * P, P), :]).then_inc(c_load, 16)
                    sp.wait_ge(c_st, t * 16 + 16)
                    hold(sp, passed["sp"])

            def load_windows(g, n, q, full=G, last=0):
                if not is_before(g, LRING):
                    sp.wait_ge(n_res, g - (LRING - 1))
                    hold(sp, passed["sp"])
                windows = full + (last > 0)
                _, rows = nc.values_load_multi_w_load_instructions(
                    row_tab[0:1, bass.ds(g * G, windows)], (mybir.EngineType.SP,), min_val=0, max_val=ROWS - SEG,
                    skip_runtime_bounds_check_because="first_row is clamped to EP - SEG or counts compacted rows")
                for j, row in enumerate(rows):
                    sp.dma_start(seg[0:SEG_P, q, j, :, :].rearrange("p c f -> p (c f)"),
                                 msgs[bass.ds(row, SEG), :].rearrange("(p c) f -> p (c f)", c=CHUNKS)
                                 ).then_inc(n_seg[q], 16)

            sweep(sp, NGW - 1, load_windows, LRING, LRING)
            g = NGW - 1
            load_windows(g, g // LRING, g % LRING, LAST_FULL, LAST)

        @block.gpsimd
        def _(pool):
            nc.gpsimd.memset(src_all[:, :], 0).then_inc(s_padded, 1)
            nc.gpsimd.memset(dst_i[:, :], DST_PAD).then_inc(s_padded, 1)
            nc.gpsimd.memset(next_i[:, :], DST_PAD).then_inc(s_padded, 1)
            nc.gpsimd.memset(type_i[:, :], 0).then_inc(s_padded, 1)
            nc.gpsimd.memset(norm_all[:, :], 0.0).then_inc(s_padded, 1)
            nc.gpsimd.memset(w_mix[:, :], 0.0).then_inc(s_padded, 1)
            nc.gpsimd.iota(iota_i[:, :], [[1, P]], base=0, channel_multiplier=0).then_inc(s_iotas, 1)
            nc.gpsimd.iota(part_i[:, :], [[0, 1]], base=0, channel_multiplier=1).then_inc(s_iotas, 1)
            nc.gpsimd.iota(win_i[:, :], [[P, NGW * G]], base=0, channel_multiplier=0).then_inc(s_iotas, 1)
            pool.wait_ge(s_src, 32)

            def add_pair(t, r):
                pool.wait_ge(s_z, t + 1)
                nc.gpsimd.tensor_tensor(u[:, r, :], z[:, r, 0, :], z[:, r, 1, :], ALU.add).then_inc(s_u, 1)

            def dst_column(g, n, q):
                if not is_before(g, RING):
                    pool.wait_ge(s_stored[q], n * 16)
                nc.gpsimd.tensor_copy(msg[:, q, :, F:C], dst_f[:, bass.ds(g * G, G)].unsqueeze(2)).then_inc(s_dst_col, 1)

            def gains(g, q):
                pool.wait_ge(s_rstd, g + 1)
                if not is_before(g, RING):
                    pool.wait_ge(s_mix, g - (RING - 1))
                nc.gpsimd.tensor_tensor(gain[:, q, :], norm_all[:, bass.ds(g * G, G)], rstd[:, q, :],
                                        ALU.mult).then_inc(s_gain, 1)

            def gathers(g, n, q):
                if not beyond(g, NG):
                    if not is_before(g, RING):
                        pool.wait_ge(s_gather[q * G + G - 1], n * 16)
                    nc.gpsimd.tensor_copy(idx[:, q, :], src_all[:, bass.ds(g * G, G)]).then_inc(s_idx, 1)
                    pool.wait_ge(s_idx, g + 1)
                    if not is_before(g, RING):
                        pool.wait_ge(s_relu, g * G - (RING - 1) * G)
                    hold(pool, passed["pool"])
                for j in range(G):
                    if not beyond(g, NG):
                        nc.gpsimd.indirect_dma_start(
                            xg[:, q, j, :], None, x, bass.IndirectOffsetOnAxis(ap=idx[:, q, j:j + 1], axis=0)
                        ).then_inc(s_gather[q * G + j], 16)
                    if j == 2 and not is_before(g, 2):
                        gains(g - 2, (q - 2) % RING)
                    if not is_before(g, 3):
                        add_pair(g * G + (j - 3 * G), (q * G + j) % RING)
                if not is_before(g, 2):
                    if is_before(g, 3):
                        pool.wait_ge(s_floats, 1)
                    dst_column(g - 2, round_before(n, q, 2), (q - 2) % RING)

            sweep(pool, NG, gathers)
            gathers(NG, NG // RING, NG % RING)
            gathers(NG + 1, (NG + 1) // RING, (NG + 1) % RING)
            for t in range((NG - 1) * G, NT):
                add_pair(t, t % RING)

            pool.wait_ge(s_table, 48)
            with pool.If(pool.value_load(mode, min_val=0, max_val=1) > 0):
                pool.wait_ge(c_zero_st, (NW + 2) * 16)
                with pool.Fori(0, NT) as t:
                    pool.wait_ge(c_idx, t + 1)
                    hold(pool, passed["pool"])
                    nc.gpsimd.indirect_dma_start(
                        ccur[:, :], None, msgs, bass.IndirectOffsetOnAxis(ap=cidx[:, :], axis=0)).then_inc(c_cur, 16)
                    pool.wait_ge(c_new, t + 1)
                    hold(pool, passed["pool"])
                    nc.gpsimd.indirect_dma_start(
                        msgs, bass.IndirectOffsetOnAxis(ap=cidx[:, :], axis=0), ccur[:, :], None).then_inc(c_st, 16)
                    pool.wait_ge(c_st, t * 16 + 16)

            def store_results(g, q, full=G, last=0):
                r = q % NRING
                pool.wait_ge(n_res, g + 1)
                hold(pool, passed["pool"])
                if full:
                    pool.dma_start(OUT_WIN[:, bass.ds(g * G, full), :], res[:, r, 0:full, :]).then_inc(n_out[r], 16)
                if last:
                    pool.dma_start(out[(NW - 1) * P:N, :], res[0:last, r, full, :]).then_inc(n_out[r], 16)

            def load_x(g, n, q, full=G, last=0):
                if not is_before(g, LRING):
                    store_results(g - LRING, q)
                if full:
                    pool.dma_start(xw[:, q, 0:full, :], X_WIN[:, bass.ds(g * G, full), :]).then_inc(n_x[q], 16)
                if last:
                    pool.dma_start(xw[0:last, q, full, :], x[(NW - 1) * P:N, :]).then_inc(n_x[q], 16)
                if not is_before(g, LAG):
                    relative(g - LAG, round_before(n, q, LAG, LRING), (q - LAG) % LRING)

            LAG = 3

            def relative(g, n, q, windows=G):
                r = q % NRING
                pool.wait_ge(n_seg[q], n * (16 * G) + 16 * windows)
                if not is_before(g, NRING):
                    pool.wait_ge(n_pick, g - (NRING - 1))
                nc.gpsimd.tensor_tensor(rel[:, r, 0:windows, :], seg[0:SEG_P, q, 0:windows, :, F],
                                        win_off[0:SEG_P, bass.ds(g * G, windows)].unsqueeze(2).to_broadcast(
                                            [SEG_P, windows, CHUNKS]), ALU.subtract).then_inc(n_rel, 1)

            sweep(pool, NGW - 1, load_x, LRING, LRING)
            last_g = NGW - 1
            load_x(last_g, last_g // LRING, last_g % LRING, LAST_FULL, LAST)
            for g in range(NGW - LRING, last_g):
                ahead = g + LRING - LAG
                if ahead < NGW:
                    relative(ahead, ahead // LRING, ahead % LRING, G if ahead < last_g else LAST_FULL + 1)
                store_results(g, g % NRING)
            store_results(last_g, last_g % NRING, LAST_FULL, LAST)
            for r in range(NRING):
                pool.wait_ge(n_out[r], 16 * (len(range(r, NGW, NRING)) + (r == last_g % NRING and LAST_FULL > 0)))

        @block.scalar
        def _(act):
            def scale_bases(g, q, j):
                t, r = g * G + j, (q * G + j) % RING
                if j == 0:
                    act.wait_ge(s_mix, g + 1)
                if not is_before(g, 1) or j >= RING:
                    act.wait_ge(s_a, g * (2 * G) + 2 * (j - RING + 1))
                act.wait_ge(s_y_high, t + 1)
                nc.scalar.activation(z[:, r, 2, :], y_ps[r][:, B // 2, :], ACT.Copy,
                                     scale=mix[:, q, j, B // 2:B // 2 + 1]).then_inc(s_z_high, 1)
                act.wait_ge(s_y, t + 1)
                for b in range(2):
                    ins = nc.scalar.activation(z[:, r, b, :], y_ps[r][:, b, :], ACT.Copy, scale=mix[:, q, j, b:b + 1])
                ins.then_inc(s_z, 1)

            def group_means(g, n, q):
                if not is_before(g, RING):
                    act.wait_ge(s_hT, g - (RING - 1))
                    act.wait_ge(s_std, g - (RING - 1))
                    act.wait_ge(s_relu, g * G - (RING - 1) * G)
                for j in range(DV, G):
                    act.wait_ge(s_gather[q * G + j], n * 16 + 16)
                    nc.scalar.activation(h[:, q, j, :], xg[:, q, j, :], ACT.Copy, scale=-1.0 / D,
                                         accum_out=neg_mean[:, q, j:j + 1]).then_inc(s_mean_act, 1)

            def group_squares(g, q):
                for j in range(DV, G):
                    act.wait_ge(s_mean_act, g * (G - DV) + (j - DV + 1))
                    nc.scalar.activation(h[:, q, j, :], xg[:, q, j, :], ACT.Square, bias=neg_mean[:, q, j:j + 1],
                                         accum_out=squares[:, q, j - DV:j - DV + 1]).then_inc(s_squares, 1)

            def step(g, n, q):
                def mixing(j):
                    if not is_before(g, 1):
                        scale_bases(g - 1, (q - 1) % RING, j)

                def normalised(tiles):
                    for j in tiles:
                        nc.scalar.activation(h[:, q, j, :], xg[:, q, j, :], ACT.Relu,
                                             bias=neg_mean[:, q, j:j + 1]).then_inc(s_relu, 1)

                mixing(0)
                act.wait_ge(s_mean, g + 1)
                act.wait_ge(s_squares, (g + 1) * (G - DV))
                if not is_before(g, RING):
                    act.wait_ge(s_hT, g - (RING - 1))
                normalised(range(0, G // 2))
                if not is_before(g, RING):
                    act.wait_ge(s_rstd, g - (RING - 1))
                nc.scalar.activation(std[:, q, 0:DV], mv[:, q, :, 1], ACT.Sqrt, bias=eps_col[:, 0:1])
                nc.scalar.activation(std[:, q, DV:G], squares[:, q, :], ACT.Sqrt, bias=eps_col[:, 0:1],
                                     scale=1.0 / D).then_inc(s_std, 1)
                mixing(1)
                normalised(range(G // 2, G))
                act.wait_ge(s_hotT, g + 1)
                if not is_before(g, RING):
                    act.wait_ge(s_mix_ps, g - (RING - 1))
                nc.scalar.activation(hotT[:, q, :], mix_ps[:, 0:P], ACT.Copy).then_inc(s_hotT_sb, 1)
                mixing(2)
                act.wait_ge(s_hT, g + 1)
                if not is_before(g, RING):
                    act.wait_ge(s_y, g * G - (RING - 1) * G)
                nc.scalar.activation(hT[:, q, :, :], hT_ps[:, :, :], ACT.Copy).then_inc(s_hT_sb, 1)
                if not beyond(g, NG - 1):
                    group_means(g + 1, round_after(n, q), (q + 1) % RING)
                mixing(3)
                if not beyond(g, NG - 1):
                    group_squares(g + 1, (q + 1) % RING)

            act.wait_ge(s_floats, 1)
            group_means(0, 0, 0)
            group_squares(0, 0)
            sweep(act, NG - 1, step)
            step(NG - 1, (NG - 1) // RING, (NG - 1) % RING)
            for j in range(G):
                scale_bases(NG - 1, (NG - 1) % RING, j)

            def window_std(g, q):
                r = q % NRING
                act.wait_ge(n_mv, g + 1)
                nc.scalar.activation(nstd[:, r, :], nmv[:, r, :, 1], ACT.Sqrt, bias=eps_col[:, 0:1]).then_inc(n_std, 1)

            def node_step(g, n, q, ahead=True):
                r = q % NRING
                act.wait_ge(n_shift, g + 1)
                if not is_before(g, NRING):
                    act.wait_ge(n_hT, g - (NRING - 1))
                for j in range(G):
                    ins = nc.scalar.activation(hw[:, r, j, :], xw[:, q, j, :], ACT.Relu, bias=shift[:, r, j:j + 1],
                                               scale=nrstd[:, r, j:j + 1])
                ins.then_inc(n_h, 1)
                if ahead:
                    window_std(g + 1, q + 1)
                act.wait_ge(n_hT, g + 1)
                if not is_before(g, NRING):
                    act.wait_ge(n_y, g - (NRING - 1))
                nc.scalar.activation(hwT[:, r, :, :], hwT_ps[q % 2], ACT.Copy).then_inc(n_hT_sb, 1)

            window_std(0, 0)
            sweep(act, NGW - 1, node_step, LRING, LRING)
            node_step(NGW - 1, (NGW - 1) // LRING, (NGW - 1) % LRING, False)

        @block.tensor
        def _(pe):
            pe.wait_ge(s_meta, 1)

            def count(t, first, last):
                return nc.tensor.matmul(mix_ps[0:HI, 256:256 + LO], hi_hot[:, :, t], lo_hot[:, :, t],
                                        start=first, stop=last)

            for t in range(NT):
                mm = count(t, t == 0, t == NT - 1)
            mm.then_inc(s_hist, 1)
            pe.wait_ge(s_weights, 16 * (3 + G))

            def products(g, q, j):
                r = (q * G + j) % RING
                if not is_before(g, 1) or j >= RING:
                    pe.wait_ge(s_a, g * (2 * G) + 2 * (j - RING + 1))
                for b0, done in ((B // 2, s_y_high), (0, s_y)):
                    nc.tensor.matmul(y_ps[r][:, b0:b0 + B // 2, :], hT[:, q, j, :],
                                     w_all[:, b0:b0 + B // 2, :], start=True, stop=True).then_inc(done, 1)

            def step(g, n, q):
                def messages(j):
                    if not is_before(g, 1):
                        if j == 0:
                            pe.wait_ge(s_hT_sb, g)
                        products(g - 1, (q - 1) % RING, j)

                messages(0)
                messages(1)
                pe.wait_ge(s_hot, g + 1)
                if not is_before(g, 1):
                    pe.wait_ge(s_mix, g)
                nc.tensor.transpose(mix_ps[:, 0:P], hot[:, q, :, :].rearrange("p t r -> p (t r)"),
                                    ident[:, :]).then_inc(s_hotT, 1)
                messages(2)
                pe.wait_ge(s_hotT_sb, g + 1)
                nc.tensor.matmul(mix_ps[:, P:P + G * B], hotT[:, q, :], w_mix[:, :],
                                 start=True, stop=True).then_inc(s_mix_ps, 1)
                pe.wait_ge(s_relu, g * G + G)
                for j in range(G):
                    mm = nc.tensor.transpose(hT_ps[:, j, :], h[:, q, j, :], ident[:, :])
                mm.then_inc(s_hT, 1)
                messages(3)

            sweep(pe, NG - 1, step)
            pe.wait_ge(s_meta, 2)
            nc.tensor.matmul(mix_ps[0:HI, 300:301], above[0:HI, 0:HI], upto[:, LO - 1:LO], start=True, stop=True)
            nc.tensor.matmul(mix_ps[:, 302:303], ones[:, :], bad[:, 3:4], start=True, stop=True).then_inc(s_off, 1)
            pe.wait_ge(s_meta, 3)
            step(NG - 1, (NG - 1) // RING, (NG - 1) % RING)
            pe.wait_ge(s_hT_sb, NG)
            for j in range(G):
                products(NG - 1, (NG - 1) % RING, j)

            pe.wait_ge(s_table, 48)
            with pe.If(pe.value_load(mode, min_val=0, max_val=1) > 0):
                with pe.Fori(0, NT) as t:
                    pe.wait_ge(c_dst, t + 1)
                    nc.tensor.transpose(hT_ps[:, 0, :], cdst[:, :], ident[:, :]).then_inc(c_row, 1)
                    pe.wait_ge(c_step, t * 7 + 1)
                    nc.tensor.matmul(mix_ps[:, 0:F], ceq[:, :], cm[:, 0:F], start=True, stop=True).then_inc(c_sum, 1)

            def window_sums(g, q, windows=G):
                r = q % NRING
                pe.wait_ge(n_hT_sb, g + 1)
                pe.wait_ge(n_pick, g + 1)
                if not is_before(g, NRING):
                    pe.wait_ge(n_res, g - (NRING - 1))
                for j in range(windows):
                    y = win_ps[r][:, j, :]
                    nc.tensor.matmul(y, hwT[:, r, j, :], w_loop[:, :], start=True, stop=False)
                    nc.tensor.matmul(y, pick[:, r, j, 0, :][0:SEG_P], seg[0:SEG_P, q, j, 0, 0:F],
                                     start=False, stop=False)
                    mm = nc.tensor.matmul(y, pick[:, r, j, 1, :][0:SEG_P + 1], seg[0:SEG_P + 1, q, j, 1, 0:F],
                                          start=False, stop=True)
                mm.then_inc(n_y, 1)

            def node_step(g, n, q):
                pe.wait_ge(n_h, g + 1)
                if not is_before(g, 2):
                    pe.wait_ge(n_hT_sb, g - 1)
                for j in range(G):
                    mm = nc.tensor.transpose(hwT_ps[q % 2][:, j, :], hw[:, q % NRING, j, :], ident[:, :])
                mm.then_inc(n_hT, 1)
                if not is_before(g, 1):
                    window_sums(g - 1, (q - 1) % LRING)

            sweep(pe, NGW, node_step, LRING, LRING)
            g = NGW - 1
            window_sums(g, g % LRING, LAST_FULL + 1)

        @block.vector
        def _(dve):
            nc.vector.memset(ones[:, :], 1.0)
            nc.vector.memset(eps_col[:, :], EPS)
            nc.vector.memset(bad[:, :], 0.0)
            nc.vector.memset(pick[SEG_P:P, :, :, :, :], 1.0)
            dve.wait_ge(s_iotas, 3)
            nc.vector.tensor_copy(iota_n[:, :], iota_i[:, :])
            nc.vector.tensor_copy(part_f[:, :], part_i[:, :])
            nc.vector.tensor_copy(win_off[:, :], win_i[:, :]).then_inc(s_step, 1)
            dve.wait_ge(s_step, 1)
            nc.vector.tensor_scalar(ident[:, :], iota_n[:, :], part_f[:, 0:1], None, ALU.is_equal)
            nc.vector.tensor_scalar(above[:, :], iota_n[:, :], part_f[:, 0:1], None, ALU.is_gt)
            nc.vector.tensor_scalar(below[:, :], iota_n[:, :], part_f[:, 0:1], None, ALU.is_lt)
            dve.wait_ge(s_edges, 16 * 8)
            nc.vector.tensor_copy(type_f[:, :], type_i[:, :])
            nc.vector.tensor_copy(next_f[:, :], next_i[:, :])
            nc.vector.tensor_copy(dst_f[:, :], dst_i[:, :]).then_inc(s_floats, 1)

            nc.vector.tensor_scalar(lo_i[:, :], dst_i[:, :], P.bit_length() - 1, LO - 1,
                                    ALU.logical_shift_right, ALU.bitwise_and)
            nc.vector.tensor_scalar(hi_i[:, :], dst_i[:, :], (P * LO).bit_length() - 1, None,
                                    ALU.logical_shift_right).then_inc(s_step, 1)
            dve.wait_ge(s_step, 2)
            nc.vector.tensor_copy(lo_b[:, :], lo_i[:, :])
            nc.vector.tensor_copy(hi_b[:, :], hi_i[:, :]).then_inc(s_step, 1)
            dve.wait_ge(s_step, 3)
            for v in range(LO):
                nc.vector.tensor_scalar(lo_hot[:, v, :], lo_b[:, :], float(v), None, ALU.is_equal)
            for v in range(HI):
                ins = nc.vector.tensor_scalar(hi_hot[:, v, :], hi_b[:, :], float(v), None, ALU.is_equal)
            ins.then_inc(s_meta, 1)
            dve.wait_ge(s_floats, 1)
            nc.vector.tensor_tensor(falls[:, 0:NT - 1], dst_f[:, 0:NT - 1], dst_f[:, 1:NT], ALU.is_gt)
            nc.vector.tensor_tensor(falls[:, NT - 1:NT], dst_f[:, NT - 1:NT], next_f[:, :],
                                    ALU.is_gt).then_inc(s_step, 1)
            dve.wait_ge(s_step, 4)
            nc.vector.tensor_reduce(bad[:, 0:1], falls[:, :], AX_X, ALU.max).then_inc(s_step, 1)

            def add(acc, r, c, base, first):
                return nc.vector.scalar_tensor_tensor(out=acc, in0=y_ps[r][:, base, :], scalar=c[:, base:base + 1],
                                                      in1=first, op0=ALU.mult, op1=ALU.add)

            def sum_high(g, q, j, base):
                r, before = (q * G + j) % RING, g * (3 * G) + 3 * j + (base - 5)
                if base == 5:
                    dve.wait_ge(s_z_high, g * G + j + 1)
                    first = z[:, r, 2, :]
                    if not is_before(g, 1) or j >= RING:
                        dve.wait_ge(s_msg, g * G + j - (RING - 1))
                else:
                    dve.wait_ge(s_b, before)
                    first = sum_b[:, r, :]
                add(sum_b[:, r, :], r, mix[:, q, j, :], base, first).then_inc(s_b, 1)

            def sum_low(g, q, j, base):
                r, before = (q * G + j) % RING, g * (2 * G) + 2 * j + (base - 2)
                if base == 2:
                    dve.wait_ge(s_u, g * G + j + 1)
                    first = u[:, r, :]
                else:
                    dve.wait_ge(s_b, g * (3 * G) + 3 * j + 3)
                    dve.wait_ge(s_a, before)
                    first = sum_a[:, r, :]
                add(sum_a[:, r, :], r, mix[:, q, j, :], base, first).then_inc(s_a, 1)

            def message(g, n, q, j):
                r = (q * G + j) % RING
                if j == 0 and not is_before(g, RING):
                    dve.wait_ge(s_stored[q], n * 16)
                dve.wait_ge(s_a, g * (2 * G) + 2 * j + 2)
                nc.vector.tensor_tensor(msg[:, q, j, 0:F], sum_a[:, r, :], sum_b[:, r, :], ALU.add).then_inc(s_msg, 1)

            def tile_slot(g, n, q, j, more):
                now = not is_before(g, 1) and not beyond(g, NG + 1)
                p = g - 1, round_before(n, q), (q - 1) % RING
                b = p if j else (g - 2, round_before(n, q, 2), (q - 2) % RING)
                bj = (j - 1) % G
                past = not is_before(g, 1 if j else 2)
                an, aq = round_after(n, q), (q + 1) % RING
                if now:
                    sum_high(p[0], p[2], j, 5)
                if past:
                    sum_low(b[0], b[2], bj, 2)
                if now:
                    sum_high(p[0], p[2], j, 6)
                if past:
                    sum_low(b[0], b[2], bj, 3)
                if more:
                    dve.wait_ge(s_gather[aq * G + j], an * 16 + 16)
                    if j == 0 and not is_before(g, RING - 1):
                        dve.wait_ge(s_bn, g * (2 * DV) - (RING - 2) * (2 * DV))
                        dve.wait_ge(s_std, g - (RING - 2))
                        dve.wait_ge(s_relu, g * G - (RING - 2) * G)
                    nc.vector.bn_stats(stats[:, aq, j, :], xg[:, aq, j, :]).then_inc(s_bn, 1)
                if now:
                    sum_high(p[0], p[2], j, 7)
                if more:
                    dve.wait_ge(s_bn, g * (2 * DV) + (2 * DV + 2 * j + 1))
                if past:
                    message(*b, bj)
                elif more:
                    hold(dve, passed["dve"])
                if more:
                    nc.vector.bn_aggr(mv[:, aq, j, :], stats[:, aq, j, :]).then_inc(s_bn, 1)

            def one_hot(g, q):
                if not is_before(g, RING):
                    dve.wait_ge(s_hotT, g - (RING - 1))
                nc.vector.tensor_tensor(hot[:, q, :, :],
                                        type_f[:, bass.ds(g * G, G)].unsqueeze(2).to_broadcast([P, G, R]),
                                        iota_n[:, 0:R].unsqueeze(1).to_broadcast([P, G, R]),
                                        ALU.is_equal).then_inc(s_hot, 1)

            def means(g, q):
                dve.wait_ge(s_bn, g * (2 * DV) + 2 * DV)
                nc.vector.tensor_scalar(neg_mean[:, q, 0:DV], mv[:, q, :, 0], -1.0, None, ALU.mult).then_inc(s_mean, 1)

            def step(g, n, q):
                more, here = not beyond(g, NG - 1), not beyond(g, NG)
                tile_slot(g, n, q, 0, more)
                tile_slot(g, n, q, 1, more)
                if here:
                    dve.wait_ge(s_std, g + 1)
                    if not is_before(g, RING):
                        dve.wait_ge(s_gain, g - (RING - 1))
                    nc.vector.reciprocal(rstd[:, q, :], std[:, q, :]).then_inc(s_rstd, 1)
                if more:
                    means(g + 1, (q + 1) % RING)
                tile_slot(g, n, q, 2, False)
                if here:
                    dve.wait_ge(s_gain, g + 1)
                    dve.wait_ge(s_mix_ps, g + 1)
                    nc.vector.tensor_tensor(mix[:, q, :, :],
                                            mix_ps[:, P:P + G * B].rearrange("p (t b) -> p t b", t=G),
                                            gain[:, q, :].unsqueeze(2).to_broadcast([P, G, B]),
                                            ALU.mult).then_inc(s_mix, 1)
                tile_slot(g, n, q, 3, False)
                if more:
                    one_hot(g + 1, (q + 1) % RING)

            for j in range(DV):
                dve.wait_ge(s_gather[j], 16)
                nc.vector.bn_stats(stats[:, 0, j, :], xg[:, 0, j, :]).then_inc(s_bn, 1)
                dve.wait_ge(s_bn, 2 * j + 1)
                nc.vector.bn_aggr(mv[:, 0, j, :], stats[:, 0, j, :]).then_inc(s_bn, 1)
            one_hot(0, 0)
            means(0, 0)
            sweep(dve, NG - 1, step)

            dve.wait_ge(s_hist, 1)
            nc.vector.tensor_copy(hist[:, :], mix_ps[0:HI, 256:256 + LO]).then_inc(s_step, 1)
            dve.wait_ge(s_step, 6)
            nc.vector.tensor_tensor_scan(upto[:, :], ones[0:HI, 0:LO], hist[:, :], 0.0, ALU.mult, ALU.add)
            nc.vector.tensor_scalar(big[:, :], hist[:, :], float(SEG), None, ALU.is_gt).then_inc(s_step, 1)
            dve.wait_ge(s_step, 7)
            nc.vector.tensor_reduce(bad[0:HI, 1:2], big[:, :], AX_X, ALU.max).then_inc(s_step, 1)
            dve.wait_ge(s_step, 8)
            nc.vector.tensor_tensor(bad[:, 3:4], bad[:, 0:1], bad[:, 1:2], ALU.add).then_inc(s_meta, 1)
            dve.wait_ge(s_off, 1)
            nc.vector.tensor_copy(before[:, :], mix_ps[0:HI, 300:301]).then_inc(s_step, 1)
            nc.vector.tensor_scalar(mode_f[:, :], mix_ps[:, 302:303], 0.5, None, ALU.is_gt).then_inc(s_meta, 1)
            nc.vector.tensor_scalar(big[:, :], part_f[0:HI, 0:1].to_broadcast([HI, LO]), float(LO * P), float(EP),
                                    ALU.mult, ALU.add)
            dve.wait_ge(s_step, 9)
            nc.vector.scalar_tensor_tensor(out=start[:, :], in0=upto[:, :], scalar=before[:, 0:1],
                                           in1=hist[:, :], op0=ALU.add, op1=ALU.subtract).then_inc(s_step, 1)
            dve.wait_ge(s_step, 10)
            nc.vector.tensor_scalar(start_c[:, :], start[:, :], float(EP - SEG), None, ALU.min)
            nc.vector.scalar_tensor_tensor(out=hist[:, :], in0=iota_n[0:HI, 0:LO], scalar=float(P),
                                           in1=big[:, :], op0=ALU.mult, op1=ALU.add).then_inc(s_step, 1)
            dve.wait_ge(s_step, 11)
            nc.vector.tensor_tensor(upto[:, :], hist[:, :], start_c[:, :], ALU.subtract).then_inc(s_step, 1)
            dve.wait_ge(s_step, 12)
            nc.vector.tensor_copy(mode_i[:, :], mode_f[:, :])
            nc.vector.scalar_tensor_tensor(out=start_i[:, :], in0=upto[:, :], scalar=mode_f[0:HI, 0:1],
                                           in1=start_c[:, :], op0=ALU.mult, op1=ALU.add).then_inc(s_start, 1)

            step(NG - 1, (NG - 1) // RING, (NG - 1) % RING)
            step(NG, NG // RING, NG % RING)
            last = NG - 1, (NG - 1) // RING, (NG - 1) % RING
            sum_low(last[0], last[2], G - 1, 2)
            sum_low(last[0], last[2], G - 1, 3)
            message(*last, G - 1)

            dve.wait_ge(s_table, 48)
            with dve.If(dve.value_load(mode, min_val=0, max_val=1) > 0):
                nc.vector.memset(cz[:, 0:F], 0.0)
                nc.vector.tensor_scalar(cz[:, F:C], part_f[:, :], -float(P), None, ALU.add).then_inc(c_own, 1)
                with dve.Fori(0, NW + 2) as w:
                    dve.wait_ge(c_own, w + 1)
                    nc.vector.tensor_scalar(cz[:, F:C], cz[:, F:C], float(P), None, ALU.add).then_inc(c_own, 1)
                    dve.wait_ge(c_own, w + 2)
                    nc.vector.tensor_copy(cc[:, 7:8], cz[:, F:C]).then_inc(c_zero, 1)
                    dve.wait_ge(c_zero_st, w * 16 + 16)
                    hold(dve, passed["dve"])
                with dve.Fori(0, NT) as t:
                    tile_dst = cm[:, F:C]
                    dve.wait_ge(c_load, t * 16 + 16)
                    nc.vector.tensor_scalar(cdst[:, :], ones[:, :], tile_dst, None, ALU.mult).then_inc(c_dst, 1)
                    dve.wait_ge(c_row, t + 1)
                    nc.vector.tensor_scalar(ceq[:, :], hT_ps[:, 0, :], tile_dst, None, ALU.is_equal).then_inc(c_step, 1)
                    nc.vector.tensor_scalar(cc[:, 1:2], tile_dst, N - 0.5, None, ALU.is_gt).then_inc(c_step, 1)
                    nc.vector.scalar_tensor_tensor(out=cc[:, 3:4], in0=part_f[:, :], scalar=float(DUMMY - EP),
                                                   in1=tile_dst, op0=ALU.add, op1=ALU.subtract).then_inc(c_step, 1)
                    dve.wait_ge(c_step, t * 7 + 3)
                    nc.vector.tensor_tensor(cwork[:, :], ceq[:, :], below[:, :], ALU.mult).then_inc(c_step, 1)
                    dve.wait_ge(c_step, t * 7 + 4)
                    nc.vector.tensor_reduce(cc[:, 0:1], cwork[:, :], AX_X, ALU.add).then_inc(c_step, 1)
                    dve.wait_ge(c_step, t * 7 + 5)
                    nc.vector.scalar_tensor_tensor(out=cc[:, 2:3], in0=cc[:, 0:1], scalar=1.0, in1=cc[:, 1:2],
                                                   op0=ALU.min, op1=ALU.max).then_inc(c_step, 1)
                    dve.wait_ge(c_step, t * 7 + 6)
                    nc.vector.tensor_tensor(cc[:, 4:5], cc[:, 2:3], cc[:, 3:4], ALU.mult).then_inc(c_step, 1)
                    dve.wait_ge(c_step, t * 7 + 7)
                    nc.vector.scalar_tensor_tensor(out=cidx[:, :], in0=tile_dst, scalar=float(EP), in1=cc[:, 4:5],
                                                   op0=ALU.add, op1=ALU.add).then_inc(c_idx, 1)
                    dve.wait_ge(c_cur, t * 16 + 16)
                    dve.wait_ge(c_sum, t + 1)
                    nc.vector.tensor_tensor(ccur[:, 0:F], ccur[:, 0:F], mix_ps[:, 0:F], ALU.add).then_inc(c_new, 1)

            def window_stats(g, n, q, tiles, x_loads=1):
                r = q % NRING
                if 0 in tiles:
                    dve.wait_ge(n_x[q], n * 16 + 16 * x_loads)
                for j in tiles:
                    nc.vector.bn_stats(nstats[:, r, j, :], xw[:, q, j, :]).then_inc(n_bn, 1)

            def window_rows(g, q, windows=G):
                r = q % NRING
                if not is_before(g, NRING):
                    dve.wait_ge(n_y, g - (NRING - 1))
                shape = [SEG_P, windows * CHUNKS, P]
                dve.wait_ge(n_rel, g + 1)
                nc.vector.tensor_tensor(
                    pick[0:SEG_P, r, 0:windows, :, :].rearrange("p j c n -> p (j c) n"),
                    iota_n[0:SEG_P, :].unsqueeze(1).to_broadcast(shape),
                    rel[:, r, 0:windows, :].rearrange("p j c -> p (j c)").unsqueeze(2).to_broadcast(shape),
                    ALU.is_equal).then_inc(n_pick, 1)

            def window_means(g, q):
                r = q % NRING
                dve.wait_ge(n_bn, g * G + G)
                hold(dve, passed["dve"])
                for j in range(G):
                    ins = nc.vector.bn_aggr(nmv[:, r, j, :], nstats[:, r, j, :])
                ins.then_inc(n_mv, 1)

            def window_rstd(g, q):
                r = q % NRING
                dve.wait_ge(n_std, g + 1)
                nc.vector.reciprocal(nrstd[:, r, :], nstd[:, r, :]).then_inc(n_rstd, 1)

            def window_shift(g, q):
                r = q % NRING
                dve.wait_ge(n_rstd, g + 1)
                nc.vector.scalar_tensor_tensor(out=shift[:, r, :], in0=nmv[:, r, :, 0], scalar=-1.0,
                                               in1=nrstd[:, r, :], op0=ALU.mult, op1=ALU.mult).then_inc(n_shift, 1)

            def results(g, n, q, windows=G):
                r = q % NRING
                dve.wait_ge(n_y, g + 1)
                if not is_before(g, NRING):
                    dve.wait_ge(n_out[r], n * (16 * LRING // NRING) + 16 * (q // NRING))
                nc.vector.scalar_tensor_tensor(out=res[:, r, 0:windows, :], in0=win_ps[r][:, 0:windows, :], scalar=0.0,
                                               in1=xw[:, q, 0:windows, :], op0=ALU.max,
                                               op1=ALU.add).then_inc(n_res, 1)

            def node_step(g, n, q, windows=G, x_loads=1):
                ahead, ahead_n, ahead_q = g + 1, round_after(n, q, LRING), (q + 1) % LRING
                window_stats(ahead, ahead_n, ahead_q, range(0, 1), x_loads)
                if not is_before(g, 2):
                    window_shift(g, q)
                window_stats(ahead, ahead_n, ahead_q, range(1, G))
                window_rows(ahead, ahead_q, windows)
                window_means(ahead, ahead_q)
                if not is_before(g, 2):
                    results(g - 2, round_before(n, q, 2, LRING), (q - 2) % LRING)
                window_rstd(ahead, ahead_q)

            for g in range(2):
                window_stats(g, 0, g, range(G))
                window_means(g, g)
                window_rstd(g, g)
                window_shift(g, g)
            for g in range(2):
                window_rows(g, g)
            sweep(dve, NGW - 2, node_step, LRING, LRING, 1)
            g = NGW - 2
            node_step(g, g // LRING, g % LRING, LAST_FULL + 1, 1 + (LAST_FULL > 0))
            window_shift(NGW - 1, (NGW - 1) % LRING)
            for g in (NGW - 3, NGW - 2):
                results(g, g // LRING, g % LRING)
            g = NGW - 1
            results(g, g // LRING, g % LRING, LAST_FULL + 1)


_INS = ["x", "src", "dst", "edge_type_32", "edge_weight1", "L0_gnn_weight", "L0_gnn_w_comp", "L0_gnn_loop_weight",
        "L0_gnn_h_bias"]


def kernel(**inputs):
    import concourse.bacc as bacc
    from concourse.bass_utils import run_bass_kernel_spmd

    nc = bacc.Bacc("TRN2", target_bir_lowering=False, num_devices=1)
    arrays, args = {}, []
    for name in _INS:
        a = np.ascontiguousarray(inputs[name])
        arrays[name] = a
        args.append(nc.dram_tensor(name, a.shape, mybir.dt.from_np(a.dtype), kind="ExternalInput").ap())
    args.append(nc.dram_tensor("out", inputs["x"].shape, F32, kind="ExternalOutput").ap())
    build_layer(nc, *args)
    r = run_bass_kernel_spmd(nc, [arrays], core_ids=[0])
    return r.results[0]["out"]
```
